# Optimizing a Trainium2 kernel written in Bass

```python
import numpy as np
import jax
import jax.numpy as jnp

def _softmax(x, axis=-1):
    return jax.nn.softmax(x, axis=axis)
def _gelu(x):
    return jax.nn.gelu(x, approximate=True)
def _silu(x):
    return jax.nn.silu(x)
def _sigmoid(x):
    return jax.nn.sigmoid(x)
def _layernorm(x, axis=-1, eps=1e-5):
    m = jnp.mean(x, axis=axis, keepdims=True)
    v = jnp.var(x, axis=axis, keepdims=True)
    return (x - m) / jnp.sqrt(v + eps)
def _scatter_add(tgt, idx, src, axis=0):
    return tgt.at[idx].add(src)
def _segment_sum(src, seg, n):
    return jax.ops.segment_sum(src, seg, n)

kernel_name = 'mk_conv_preact_d2_conv_nchw256_0dce19'

def setup_inputs(seed: int = 0):
    np.random.seed(seed)
    _w = jnp.asarray
    def _rec_inputs():
        import jax
        import jax.numpy as jnp
        _gk = jax.random.key(seed)
        x = -0.0003929 + 0.9999 * jax.random.normal(jax.random.fold_in(_gk, 1), (16, 256, 64, 64), jnp.float32)
        return x
    x = _rec_inputs()
    def _L0_conv_setup():
        import jax, jax.numpy as jnp
        import numpy as np
        HEADS = 4
        HEAD_DIM = 32
        DIM = 256
        HIDDEN = HEADS * HEAD_DIM
        SCALE = HEAD_DIM ** (-0.5)

        def rmsnorm(x, g):
            inv = jax.lax.rsqrt(jnp.sum(x * x, axis=1, keepdims=True) + 1e-12)
            return x * inv * (g * x.shape[1] ** 0.5)[None, :, None, None]
        key = jax.random.key(seed)
        k1, k2, k3 = jax.random.split(key, 3)
        b, H, W = (16, 64, 64)
        x = jax.random.normal(k1, (b, DIM, H, W), dtype=jnp.float32)
        W_qkv = jax.random.normal(k2, (3 * HIDDEN, DIM), dtype=jnp.float32) * DIM ** (-0.5)
        W_out = jax.random.normal(k3, (DIM, HIDDEN), dtype=jnp.float32) * HIDDEN ** (-0.5)
        b_out = jnp.zeros((DIM,), dtype=jnp.float32)
        g_norm = jnp.ones((DIM,), dtype=jnp.float32)
        g_out = jnp.ones((DIM,), dtype=jnp.float32)
        return {'x': x, 'W_qkv': W_qkv, 'W_out': W_out, 'b_out': b_out, 'g_norm': g_norm, 'g_out': g_out}
    _L0_conv_all = _L0_conv_setup()
    _L0_conv_in = {k: v for k, v in _L0_conv_all.items() if k in ('W_qkv', 'W_out', 'b_out', 'g_norm', 'g_out', )}
    del _L0_conv_all

    def _L1_conv_setup():
        import jax, jax.numpy as jnp
        import numpy as np
        DIM = 8
        HEADS_EFF = 64
        G = 96
        ATT_EPS = 1e-15
        BN_EPS = 1e-05

        def _conv1x1(x, w):
            return jnp.einsum('oc,bchw->bohw', w, x)
        key = jax.random.key(seed)
        ks = jax.random.split(key, 6)
        s = 0.05
        return {'x': jax.random.normal(ks[0], (8, 256, 64, 64), dtype=jnp.float32), 'w_qkv': jax.random.normal(ks[1], (768, 256), dtype=jnp.float32) * s, 'w_dw': jax.random.normal(ks[2], (768, 1, 5, 5), dtype=jnp.float32) * s, 'w_pw': jax.random.normal(ks[3], (96, 8, 8), dtype=jnp.float32) * s, 'w_proj': jax.random.normal(ks[4], (256, 512), dtype=jnp.float32) * s, 'bn_gamma': jnp.ones((256,), jnp.float32), 'bn_beta': jnp.zeros((256,), jnp.float32), 'bn_mean': jnp.zeros((256,), jnp.float32), 'bn_var': jnp.ones((256,), jnp.float32)}
    _L1_conv_all = _L1_conv_setup()
    _L1_conv_in = {k: v for k, v in _L1_conv_all.items() if k in ('w_qkv', 'w_dw', 'w_pw', 'w_proj', 'bn_gamma', 'bn_beta', 'bn_mean', 'bn_var', )}
    del _L1_conv_all

    return {
        "x": x,
        "L0_conv_W_qkv": _L0_conv_in["W_qkv"],
        "L0_conv_W_out": _L0_conv_in["W_out"],
        "L0_conv_b_out": _L0_conv_in["b_out"],
        "L0_conv_g_norm": _L0_conv_in["g_norm"],
        "L0_conv_g_out": _L0_conv_in["g_out"],
        "L1_conv_w_qkv": _L1_conv_in["w_qkv"],
        "L1_conv_w_dw": _L1_conv_in["w_dw"],
        "L1_conv_w_pw": _L1_conv_in["w_pw"],
        "L1_conv_w_proj": _L1_conv_in["w_proj"],
        "L1_conv_bn_gamma": _L1_conv_in["bn_gamma"],
        "L1_conv_bn_beta": _L1_conv_in["bn_beta"],
        "L1_conv_bn_mean": _L1_conv_in["bn_mean"],
        "L1_conv_bn_var": _L1_conv_in["bn_var"],
    }

def reference(x, L0_conv_W_qkv, L0_conv_W_out, L0_conv_b_out, L0_conv_g_norm, L0_conv_g_out, L1_conv_w_qkv, L1_conv_w_dw, L1_conv_w_pw, L1_conv_w_proj, L1_conv_bn_gamma, L1_conv_bn_beta, L1_conv_bn_mean, L1_conv_bn_var):
    import jax
    import jax.numpy as jnp
    def _L0_conv_ref(x, W_qkv, W_out, b_out, g_norm, g_out):
        import jax, jax.numpy as jnp
        import numpy as np
        HEADS = 4
        HEAD_DIM = 32
        DIM = 256
        HIDDEN = HEADS * HEAD_DIM
        SCALE = HEAD_DIM ** (-0.5)

        def rmsnorm(x, g):
            inv = jax.lax.rsqrt(jnp.sum(x * x, axis=1, keepdims=True) + 1e-12)
            return x * inv * (g * x.shape[1] ** 0.5)[None, :, None, None]
        b, c, H, W = x.shape
        n = H * W
        xn = rmsnorm(x, g_norm)
        qkv = jnp.einsum('bchw,oc->bohw', xn, W_qkv)
        qkv = qkv.reshape(b, 3, HEADS, HEAD_DIM, n)
        q, k, v = (qkv[:, 0], qkv[:, 1], qkv[:, 2])
        q = jax.nn.softmax(q, axis=-2)
        k = jax.nn.softmax(k, axis=-1)
        context = jnp.einsum('bhdn,bhen->bhde', k, v)
        out = jnp.einsum('bhde,bhdn->bhen', context, q) * SCALE
        out = out.reshape(b, HIDDEN, H, W)
        out = jnp.einsum('bchw,oc->bohw', out, W_out) + b_out[None, :, None, None]
        return rmsnorm(out, g_out)

    def _L1_conv_ref(x, w_qkv, w_dw, w_pw, w_proj, bn_gamma, bn_beta, bn_mean, bn_var):
        import jax, jax.numpy as jnp
        import numpy as np
        DIM = 8
        HEADS_EFF = 64
        G = 96
        ATT_EPS = 1e-15
        BN_EPS = 1e-05

        def _conv1x1(x, w):
            return jnp.einsum('oc,bchw->bohw', w, x)
        B, _, H, W = x.shape
        hw = H * W
        qkv = _conv1x1(x, w_qkv)
        dw = jax.lax.conv_general_dilated(qkv, w_dw, window_strides=(1, 1), padding=[(2, 2), (2, 2)], dimension_numbers=('NCHW', 'OIHW', 'NCHW'), feature_group_count=768)
        dwg = dw.reshape(B, G, 768 // G, H, W)
        agg = jnp.einsum('goi,bgihw->bgohw', w_pw, dwg).reshape(B, 768, H, W)
        ms = jnp.concatenate([qkv, agg], axis=1)
        t = ms.reshape(B, HEADS_EFF, 3 * DIM, hw).transpose(0, 1, 3, 2)
        q = jax.nn.relu(t[..., :DIM])
        k = jax.nn.relu(t[..., DIM:2 * DIM])
        v = t[..., 2 * DIM:]
        v = jnp.pad(v, ((0, 0), (0, 0), (0, 0), (0, 1)), constant_values=1.0)
        kv = jnp.einsum('bhnd,bhne->bhde', k, v)
        out = jnp.einsum('bhnd,bhde->bhne', q, kv)
        out = out[..., :-1] / (out[..., -1:] + ATT_EPS)
        out = out.transpose(0, 1, 3, 2).reshape(B, HEADS_EFF * DIM, H, W)
        proj = _conv1x1(out, w_proj)
        inv = bn_gamma / jnp.sqrt(bn_var + BN_EPS)
        return proj * inv[None, :, None, None] + (bn_beta - bn_mean * inv)[None, :, None, None]

    def _gn(v, G=32, eps=1e-5):
        B_, C_, H_, W_ = v.shape
        g = v.reshape(B_, G, C_ // G, H_, W_)
        m = jnp.mean(g, axis=(2, 3, 4), keepdims=True)
        s = jnp.var(g, axis=(2, 3, 4), keepdims=True)
        return ((g - m) / jnp.sqrt(s + eps)).reshape(v.shape)

    def _ln_c(v, eps=1e-6):
        m = jnp.mean(v, axis=1, keepdims=True)
        s = jnp.var(v, axis=1, keepdims=True)
        return (v - m) / jnp.sqrt(s + eps)

    def _ln_t(v, eps=1e-5):
        m = jnp.mean(v, axis=-1, keepdims=True)
        s = jnp.var(v, axis=-1, keepdims=True)
        return (v - m) / jnp.sqrt(s + eps)

    def _to_tokens(v):
        B_, C_, H_, W_ = v.shape
        return v.reshape(B_, C_, H_ * W_).transpose(0, 2, 1)
    def _from_tokens(t, like):
        B_, C_, H_, W_ = like.shape
        return t.transpose(0, 2, 1).reshape(B_, C_, H_, W_)

    x = x + _L0_conv_ref(_gn(x), L0_conv_W_qkv, L0_conv_W_out, L0_conv_b_out, L0_conv_g_norm, L0_conv_g_out)
    x = x + _L1_conv_ref(_gn(x), L1_conv_w_qkv, L1_conv_w_dw, L1_conv_w_pw, L1_conv_w_proj, L1_conv_bn_gamma, L1_conv_bn_beta, L1_conv_bn_mean, L1_conv_bn_var)
    return x


_drawn_inputs = setup_inputs


def setup_inputs(seed=0):
    import zlib

    import numpy as np

    out = dict(_drawn_inputs(seed))
    spreads = {'L0_conv_b_out': (0.0, 0.1),
     'L0_conv_g_norm': (1.0, 0.6),
     'L0_conv_g_out': (1.0, 0.2),
     'L1_conv_bn_gamma': (1.0, 0.2),
     'L1_conv_bn_beta': (0.0, 0.1),
     'L1_conv_bn_mean': (0.0, 0.1),
     'L1_conv_bn_var': (1.0, 0.537)}
    factors = {'L1_conv_w_dw': 5.04, 'L1_conv_w_pw': 4.912}
    for name, (base, spread) in spreads.items():
        noise = np.random.default_rng([zlib.crc32(name.encode()), seed]).standard_normal(out[name].shape)
        drawn = base * np.exp(spread * noise) if base else spread * noise
        out[name] = jnp.asarray(drawn.astype(out[name].dtype))
    for name, factor in factors.items():
        out[name] = (out[name] * factor).astype(out[name].dtype)
    return out
```

```python
from contextlib import ExitStack
import math

import numpy as np
import concourse.bass as bass
from concourse import mybir

F32, F16 = mybir.dt.float32, mybir.dt.float16
ALU, ACT = mybir.AluOpType, mybir.ActivationFunctionType
AX = mybir.AxisListType.X
RMAX = bass.bass_isa.ReduceOp.max

IMAGES, CH, H, W = 16, 256, 64, 64
N = H * W
P = 128
KT = CH // P
C = 512
NC = N // C
HALF = N // 2
TP = 124
DU = 9
HEADS0, D0 = 4, 32
HID = HEADS0 * D0
D1 = 8
PAIRS = 2
QUADS = 4
TY = 3
TAPS = 5
RB = 4
NB = H // RB
WP = W + TAPS - 1
GCOL = TAPS * D1 * RB
CONVS = QUADS * TY
SLOTS = CONVS + 2 * TY
WS = 1024.0
XS0, XS1 = 1024.0, 64.0
PROJ = 1.0 / (WS * XS1)

CI, CONE, CG8, CM32, CM8, CMGT, CTS, CSEL = (128 * j for j in range(8))
CSC = CSEL + 32
E_RMS, E_DEN, E_GN, L_XS0, L_RMS, CNUM = range(6)


def constants():
    a = np.zeros((P, CSC + CNUM), np.float32)
    r = np.arange(P)
    a[:, CI:CI + P] = r[:, None] == r
    a[:, CONE:CONE + P] = 1.0
    a[:, CG8:CG8 + P] = (r[:, None] // 8 == r // 8) / 8.0
    a[:, CM32:CM32 + P] = r[:, None] // D0 == r // D0
    a[:, CM8:CM8 + P] = r[:, None] // D1 == r // D1
    head, row, chan = r // 32, r % RB, r // RB
    a[:, CMGT:CMGT + P] = (head[:, None] == head) & (row[:, None] == row)
    a[:, CTS:CTS + P] = chan[:, None] == chan
    a[:, CSEL:CSEL + 32] = chan[:, None] == np.arange(32)
    a[:, CSC:] = [1e-12, 1e-15, 1e-5, math.log(XS0), math.log(CH ** 0.5)]
    return a




def bc(ap, shape):
    return ap.broadcast_to(shape)


def two_layers(nc, x, cst, w0t, vecs, woutt, w1t, pwp, dwp, wpd, wpa, out):
    ctx = ExitStack()
    with ctx:
        def sb(name, shape, dt=F32):
            return ctx.enter_context(nc.sbuf_tensor(name, shape, dt))

        def sem(name):
            return ctx.enter_context(nc.semaphore(name))

        w1_d = nc.dram_tensor("w1_split", (PAIRS, P, 2 * KT * TY * P), F16, kind="Internal").ap()
        wc_d = nc.dram_tensor("wc_split", (PAIRS * CONVS, P, 4 * 2 * GCOL), F16, kind="Internal").ap()

        X = sb("X", [P, KT, N])
        XN = sb("XN", [P, 2, KT, N], F16)
        QKV = sb("QKV", [P, TY, 2, RB, NB + 1, WP], F16)
        CT = sb("CT", [P, 2, 4, NB * WP], F16)
        CW = sb("CW", [P, 2, 4, 2, TAPS, 32], F16)
        OK = sb("OK", [P, 2 * C])
        OV = sb("OV", [P, 2 * C])
        OQ = sb("OQ", [P, 2, 2 * C])
        QA = sb("QA", [P, RB, 2 * C])
        KTb = sb("KTb", [P, 2, 4, P])
        VTb = sb("VTb", [P, 2, 4, P + 1])
        DN = sb("DN", [P, 2, C])
        W0 = sb("W0", [P, 2, KT, 3 * HID], F16)
        W1 = sb("W1", [P, 2, KT, TY, P], F16)
        WOUT = sb("WOUT", [P, CH])
        WPD = sb("WPD", [P, PAIRS, CH])
        WPA = sb("WPA", [P, 2, CH])
        CO = sb("CO", [P, CSC + CNUM])
        I16 = sb("I16", [P, P], F16)
        PD = sb("PD", [P, CH])
        PA = sb("PA", [P, CH])
        KVM = sb("KVM", [P, P])
        KVS = sb("KVS", [P, P])
        DM = sb("DM", [P, P])
        DMD = sb("DMD", [P, P])
        KS = sb("KS", [P, 2])
        ST = sb("ST", [P, KT, NC, 6])
        MV = sb("MV", [P, KT, 2])
        G4 = sb("G4", [P, 4, 2])
        RS = sb("RS", [P, KT])
        NBI = sb("NBI", [P, KT])
        VEC = sb("VEC", [P, 10, KT])
        MX = sb("MX", [P, 3, 4])
        KSC = sb("KSC", [P, 1])
        SCA = sb("SCA", [P, 1])
        KMX = sb("KMX", [P, NC])
        KB = sb("KB", [P, 2])
        SK = sb("SK", [P, 4])
        QX = sb("QX", [P, 2, 4, HEADS0])
        QSM = sb("QSM", [P, 2, 4, HEADS0])
        QR = sb("QR", [P, 2, 4, HEADS0])

        flat = QKV[:, :, :, :, :, :].rearrange("p a b c d e -> p (a b c d e)").bitcast(F32)
        KBUF, QS, VT = (flat[:, j * N:(j + 1) * N] for j in range(3))
        EKT = KTb
        ctf = CT[:, :, :, :].rearrange("p a b c -> p (a b c)").bitcast(F32)
        HB = ctf[:, 0:3 * KT * C].rearrange("p (s k n) -> p s k n", s=3, k=KT)
        qaf = QA[:, :, :].rearrange("p a b -> p (a b)")
        SQ = qaf[:, 0:2 * C].rearrange("p (k n) -> p k n", k=KT)
        SQS = qaf[:, 2 * C:4 * C].rearrange("p (s n) -> p s n", s=2)
        INV = qaf[:, 4 * C:6 * C].rearrange("p (s n) -> p s n", s=2)
        QM = qaf[:, 6 * C:8 * C].rearrange("p (s n) -> p s n", s=2)
        MM = OV[:, 0:CH]
        SM = OV[:, CH:CH + P]
        QF = OK[:, :].rearrange("p (s n) -> p s n", s=2)
        QN = OV[:, :].rearrange("p (s n) -> p s n", s=2)
        W0F = XN[:, 0, 0, :].bitcast(F32)[:, 0:KT * 3 * HID].rearrange("p (k n) -> p k n", k=KT)
        W1F = XN[:, 1, :, :].rearrange("p k n -> p (k n)").bitcast(F32)[:, 0:KT * TY * 2 * P].rearrange("p (k n) -> p k n", k=KT)
        W1S = XN[:, 0, 1, 0:KT * TY * 2 * P * 2].rearrange("p (q h k n) -> p q h k n", q=PAIRS, h=2, k=KT) if N >= KT * TY * 2 * P * 2 else X[:, 1, :].bitcast(F16)[:, 0:KT * TY * 2 * P * 2].rearrange("p (q h k n) -> p q h k n", q=PAIRS, h=2, k=KT)
        PW = flat[:, 0:96 * 8]
        DW = flat[:, 1024:1024 + 96 * 20]
        TF = flat[:, 4096:4096 + 2 * 4 * GCOL].rearrange("p (s g n) -> p s g n", s=2, g=4)

        PS = ctx.enter_context(nc.psum_tensor("PS", [P, 8, C], F32))

        ident, ones, g8 = CO[:, CI:CI + P], CO[:, CONE:CONE + P], CO[:, CG8:CG8 + P]
        m32, m8, mgt = CO[:, CM32:CM32 + P], CO[:, CM8:CM8 + P], CO[:, CMGT:CMGT + P]
        tsum, sel = CO[:, CTS:CTS + P], CO[:, CSEL:CSEL + 32]

        def const(j):
            return CO[:, CSC + j:CSC + j + 1]

        s_load = sem("s_load"); s_set = sem("s_set"); s_seta = sem("s_seta"); s_allmax = sem("s_allmax")
        s_hiw = sem("s_hiw"); s_tw = sem("s_tw"); s_low = sem("s_low"); s_wc = [sem(f"s_wc{j}") for j in range(2)]; s_w1s = sem("s_w1s")
        s_x = [sem(f"s_xin{h}") for h in range(2)]
        s_out = [sem(f"s_out{h}") for h in range(2)]; s_w1f = sem("s_w1f")
        s_dchain = sem("s_dchain"); s_pchain = sem("s_pchain"); s_setg = sem("s_setg")
        s_bn = sem("s_bn"); s_gin = sem("s_gin"); s_gavg = sem("s_gavg"); s_gvar = sem("s_gvar")
        s_grs = sem("s_grs"); s_gn = sem("s_gn"); s_gln = sem("s_gln")
        s_h = sem("s_h"); s_sq = sem("s_sq"); s_sqs = sem("s_sqs"); s_ss = sem("s_ss"); s_ln = sem("s_ln")
        s_inv = sem("s_inv"); s_xn = sem("s_xn"); s_hi = sem("s_hi"); s_lo = sem("s_lo")
        s_kp = sem("s_kp"); s_vp = sem("s_vp"); s_qp = sem("s_qp")
        s_kmx = sem("s_kmx"); s_kc = sem("s_kc"); s_vc = sem("s_vc"); s_qmx = sem("s_qmx"); s_qsub = sem("s_qsub")
        s_qe = sem("s_qe"); s_qsum = sem("s_qsum"); s_qr = sem("s_qr"); s_qn = sem("s_qn"); s_qt = sem("s_qt"); s_qs = sem("s_qs")
        s_kb = sem("s_kb"); s_ke = sem("s_ke"); s_ket = sem("s_ket"); s_ekt = sem("s_ekt")
        s_ctx = sem("s_ctx"); s_sm = sem("s_sm"); s_mp = sem("s_mp"); s_mm = sem("s_mm"); s_sk = sem("s_sk")
        s_y = sem("s_y"); s_yb = sem("s_yb"); s_ysq = sem("s_ysq"); s_ysqs = sem("s_ysqs"); s_yss = sem("s_yss")
        s_yln = sem("s_yln"); s_yinv = sem("s_yinv"); s_yn = sem("s_yn"); s_x1 = sem("s_x1")
        s_pad = sem("s_pad"); s_hi1 = sem("s_hi1"); s_lo1 = sem("s_lo1"); s_h1 = sem("s_h1"); s_bias = sem("s_bias")
        s_w1 = sem("s_w1"); s_pj = sem("s_pj"); s_phi = sem("s_phi"); s_plo = sem("s_plo")
        s_dt = sem("s_dt"); s_dk = sem("s_dk"); s_dv = sem("s_dv"); s_dkv = sem("s_dkv")
        s_dkm = sem("s_dkm"); s_dtr = sem("s_dtr"); s_dks = sem("s_dks"); s_dp = sem("s_dp"); s_pd = sem("s_pd")
        s_cw = [sem(f"s_cw{j}") for j in range(2)]
        s_ct = [sem(f"s_ct{j}") for j in range(2)]
        s_conv = sem("s_conv"); s_ev = [sem(f"s_ev{j}") for j in range(TY)]
        s_at = sem("s_at"); s_ak = sem("s_ak"); s_av = sem("s_av"); s_akv = sem("s_akv"); s_kvm = sem("s_kvm")
        s_sel = sem("s_sel"); s_kvs = sem("s_kvs"); s_p = sem("s_p"); s_pa = sem("s_pa"); s_wpa = [sem(f"s_wpa{j}") for j in range(2)]
        s_den = sem("s_den"); s_dln = sem("s_dln"); s_dex = sem("s_dex"); s_qd = sem("s_qd"); s_qa = [sem(f"s_qa{j}") for j in range(2)]
        s_qf = sem("s_qf"); s_qrl = sem("s_qrl"); s_fd = sem("s_fd"); s_fln = sem("s_fln"); s_fex = sem("s_fex")
        s_fq = sem("s_fq"); s_fo = sem("s_fo"); s_fin = sem("s_fin"); s_one = sem("s_one"); s_gate = sem("s_gate")

        x_v = x.rearrange("i (k p) n -> i p k n", p=P)
        out_v = out.rearrange("i (k p) n -> i p k n", p=P)

        block = ctx.enter_context(nc.Block())

        def gate(eng, semaphore, value):
            eng.wait_ge(semaphore, value)
            eng.sem_inc(s_gate, 1)

        def slot_steps(n):
            q = n // TY
            steps = {0: [("sel", q - 2, 0), ("trans", q - 1, 0)],
                     1: [("p", q - 2, 0), ("den", q - 2, 0), ("kv", q - 1, 0), ("trans", q - 1, 1)],
                     2: [("den", q - 2, 1), ("kv", q - 1, 1)]}[n % TY]
            return [s for s in steps if 0 <= s[1] < QUADS]

        def rows(ap, b0, nb, t):
            return ap.rearrange("p (b t w) -> p b t w", t=RB, w=W)[:, b0:b0 + nb, t, :]

        def padded(ty, part, b0, nb, t):
            return QKV[:, ty, part, (t + 2) % RB, b0 + (t + 2) // RB:b0 + (t + 2) // RB + nb, 2:2 + W]

        def stretch(ty, part, ci):
            t = ci // DU
            at = (WP + NB * WP - DU * TP if t < 2 else 0) + TP * (ci % DU)
            return QKV[:, ty, part, t, :, :].rearrange("p b w -> p (b w)")[:, at:at + TP]

        HB8 = C // W

        @block.sync
        def _(sp):
            ld = [(CO[:, :], cst), (W0F, w0t.rearrange("(k p) n -> p k n", p=P)),
                  (W1F, w1t.rearrange("(k p) n -> p k n", p=P)), (PW, pwp), (DW, dwp), (WOUT[:, :], woutt),
                  (WPD[:, :, :], wpd.rearrange("q p n -> p q n"))]
            ld += [(VEC[:, 0:7, :], vecs)]
            for d, s in ld:
                sp.dma_start(d, s).then_inc(s_load, 16)
            for n in range(PAIRS * CONVS):
                sp.wait_ge(s_low, n + 1)
                sp.dma_start(wc_d[n], CW[:, n % 2, :, :, :, :].rearrange("p g h x m -> p (g h x m)")).then_inc(s_wc[n % 2], 16)
            for q in range(PAIRS):
                sp.wait_ge(s_w1f, q + 1)
                sp.dma_start(w1_d[q], W1S[:, q, :, :, :].rearrange("p h k n -> p (h k n)")).then_inc(s_w1s, 16)
            sp.wait_ge(s_w1s, 16 * PAIRS)
            for m in range(2):
                sp.wait_ge(s_wc[m], 16 * PAIRS * CONVS // 2)
            with sp.Fori(0, IMAGES) as img:
                for h in range(2):
                    sp.wait_ge(s_out[h], img * 16 + 16)
                    sp.dma_start(X[:, :, h * HALF:(h + 1) * HALF], x_v[img, :, :, h * HALF:(h + 1) * HALF]).then_inc(s_x[h], 16)
                with sp.Fori(0, PAIRS) as pair:
                    pp = img * PAIRS + pair
                    sp.wait_ge(s_pj, pp * TY * NC + 1)
                    sp.dma_start(W1[:, :, :, :, :].rearrange("p h k t n -> p (h k t n)"), w1_d[pair]).then_inc(s_w1, 16)
                    for n in range(CONVS):
                        q, ty = n // TY, n % TY
                        sp.wait_ge(s_conv, pp * CONVS + n + 1)
                        sp.dma_start(CW[:, n % 2, :, :, :, :].rearrange("p g h x m -> p (g h x m)"),
                                     wc_d[pair * CONVS + n]).then_inc(s_cw[n % 2], 16)
                        if q == 0:
                            sp.wait_ge(s_plo, pp * TY * NC + (ty + 1) * NC)
                        for g in range(4):
                            src = QKV[32 * q + 8 * g:32 * q + 8 * g + 8, ty, :, :, :, :]
                            for half in range(2):
                                sp.dma_start(CT[64 * half:64 * half + 64, n % 2, g, :],
                                             src[:, :, :, half:half + NB, :].rearrange("c h t b w -> c (h t) (b w)")
                                             ).then_inc(s_ct[n % 2], 16)
                        if ty == 0:
                            sp.wait_ge(s_p, pp * QUADS + q + 1)
                            sp.dma_start(WPA[:, q % 2, :], wpa[pair * QUADS + q]).then_inc(s_wpa[q % 2], 16)
                for h in range(2):
                    sp.wait_ge(s_fin, (img * PAIRS + 1) * 2 * NC + (h + 1) * NC + 1)
                    sp.dma_start(out_v[img, :, :, h * HALF:(h + 1) * HALF], X[:, :, h * HALF:(h + 1) * HALF]).then_inc(s_out[h], 16)
            for h in range(2):
                sp.wait_ge(s_out[h], 16 * IMAGES + 16)

        @block.gpsimd
        def _(pool):
            pool.wait_ge(s_set, 1)
            pool.partition_all_reduce(MX[:, 1, :], MX[:, 0, :], P, RMAX).then_inc(s_allmax, 1)
            pool.memset(VTb[:, :, :, P:P + 1], 1.0).then_inc(s_one, 1)

            def affine(c, s, signal):
                for k in range(KT):
                    pool.tensor_scalar(HB[:, s, k, :], X[:, k, c * C:(c + 1) * C], RS[:, k:k + 1], NBI[:, k:k + 1],
                                       ALU.mult, ALU.add).then_inc(signal, 1)

            with pool.Fori(0, IMAGES) as img:
                gate(pool, s_gn, img * 2 + 1)
                for c in range(-2, NC):
                    if 0 <= c + 1 < NC:
                        if c + 1 >= 3:
                            gate(pool, s_lo, img * NC + c - 1)
                        affine(c + 1, (c + 1) % 3, s_h)
                    if c + 2 < NC:
                        pool.wait_ge(s_sq, img * 2 * NC + 2 * (c + 2) + 2)
                        if c >= 0:
                            pool.wait_ge(s_ss, img * NC + c + 1)
                        pool.tensor_tensor(SQS[:, c % 2, :], SQ[:, 0, :], SQ[:, 1, :], ALU.add).then_inc(s_sqs, 1)
                for c in range(NC + 2):
                    if c < NC:
                        pool.wait_ge(s_ysq, img * 2 * NC + 2 * c + 2)
                        if c >= 2:
                            pool.wait_ge(s_yss, img * NC + c - 1)
                        pool.tensor_tensor(SQS[:, c % 2, :], SQ[:, 0, :], SQ[:, 1, :], ALU.add).then_inc(s_ysqs, 1)
                    d = c - 2
                    if d >= 0:
                        xs = X[:, :, d * C:(d + 1) * C]
                        pool.wait_ge(s_yn, img * NC + d + 1)
                        pool.tensor_tensor(xs, HB[:, d % 3, :, :], xs, ALU.add).then_inc(s_x1, 1)
                gate(pool, s_gn, img * 2 + 2)
                for c in range(NC):
                    if c >= 3:
                        gate(pool, s_lo1, img * NC + c - 2)
                    affine(c, c % 3, s_h1)
                for ty in range(TY):
                    for t in range(RB):
                        row = QKV[:, ty, :, t, :, :]
                        pool.memset(row[:, :, :, 0:2], 0.0).then_inc(s_pad, 1)
                        pool.memset(row[:, :, :, WP - 2:WP], 0.0).then_inc(s_pad, 1)
                        edge = 0 if t < 2 else NB
                        pool.memset(row[:, :, edge, 2:2 + W], 0.0).then_inc(s_pad, 1)
                gate(pool, s_h1, (img + 1) * KT * NC)
                for k in range(KT):
                    pool.tensor_scalar(X[:, k, :], X[:, k, :], VEC[:, 8, k:k + 1], None, ALU.add).then_inc(s_bias, 1)
                with pool.Fori(0, PAIRS) as pair:
                    pp = img * PAIRS + pair
                    for n in range(SLOTS):
                        for what, q, h in slot_steps(n):
                            if what == "den":
                                pool.wait_ge(s_dex, pp * 2 * QUADS + 2 * q + h + 1)
                                part = OQ[:, q % 2, h * C:(h + 1) * C]
                                pool.tensor_tensor(part, part, DN[:, h, :], ALU.mult).then_inc(s_qd, 1)
                    for c in range(NC):
                        t, bh = c % RB, c // RB
                        if c >= 2:
                            pool.wait_ge(s_fd, pp * NC + c - 1)
                            pool.wait_ge(s_fq, pp * NC + c - 1)
                        else:
                            pool.wait_ge(s_at, pp * 2 * QUADS + 2 * QUADS)
                        pool.tensor_tensor(QF[:, c % 2, :].rearrange("p (b w) -> p b w", w=W),
                                           padded(2, 0, HB8 * bh, HB8, t), padded(2, 1, HB8 * bh, HB8, t),
                                           ALU.add).then_inc(s_qf, 1)

        def attend0(act, img, d):
            cols = slice(d * C, (d + 1) * C)
            act.wait_ge(s_kmx, img * NC + d + 1)
            act.activation(KBUF[:, cols], PS[:, 2 + d % 2, :], ACT.Copy).then_inc(s_kc, 1)
            act.wait_ge(s_vp, img * NC + d + 1)
            act.activation(VT[:, cols], PS[:, 5, :], ACT.Copy, scale=KSC[:, 0:1]).then_inc(s_vc, 1)
            act.wait_ge(s_qsub, img * NC + d + 1)
            act.activation(QM[:, d % 2, :], QM[:, d % 2, :], ACT.Exp, scale=KSC[:, 0:1]).then_inc(s_qe, 1)

        @block.scalar
        def _(act):
            act.preload_act_table_set("natural_log_exp_and_others")
            for h in range(2):
                act.sem_inc(s_out[h], 16)
            act.wait_ge(s_load, 16 * 8)
            act.activation(I16[:, :], ident, ACT.Copy).then_inc(s_seta, 1)
            act.activation(VEC[:, 7, :], VEC[:, 6, :], ACT.Ln, bias=const(E_GN)).then_inc(s_seta, 1)
            act.wait_ge(s_seta, 2)
            act.activation(VEC[:, 7, :], VEC[:, 7, :], ACT.Exp, scale=-0.5).then_inc(s_seta, 1)
            for n in range(PAIRS * CONVS):
                act.wait_ge(s_tw, 4 * (n + 1))
                if n >= 2:
                    act.wait_ge(s_wc[n % 2], 16 * (n // 2))
                act.activation(CW[:, n % 2, :, 0, :, :].rearrange("p g x m -> p g (x m)"), TF[:, n % 2, :, :], ACT.Copy).then_inc(s_hiw, 1)

            def rstd(count):
                act.wait_ge(s_gvar, count)
                act.activation(RS[:, :], G4[:, 2, :], ACT.Ln, bias=const(E_GN)).then_inc(s_gln, 1)
                act.wait_ge(s_gln, count)
                act.activation(RS[:, :], RS[:, :], ACT.Exp, scale=-0.5).then_inc(s_grs, 1)

            def rms(c, img, ready, ln, inv, used, shift):
                act.wait_ge(ready, img * NC + c + 1)
                if c >= 2:
                    act.wait_ge(used, img * NC + c - 1)
                act.activation(INV[:, c % 2, :], PS[:, c % 2, :], ACT.Ln, bias=const(E_RMS)).then_inc(ln, 1)
                act.wait_ge(ln, img * NC + c + 1)
                act.activation(INV[:, c % 2, :], INV[:, c % 2, :], ACT.Exp, scale=-0.5, bias=const(shift)).then_inc(inv, 1)

            with act.Fori(0, IMAGES) as img:
                rstd(img * 2 + 1)
                act.wait_ge(s_gn, img * 2 + 1)
                for c in range(-2, NC + 5):
                    if 0 <= c - 3 < NC:
                        attend0(act, img, c - 3)
                    if 0 <= c - 5 < NC:
                        act.wait_ge(s_qt, img * NC + c - 4)
                        act.activation(QS[:, (c - 5) * C:(c - 4) * C], PS[:, 6, :], ACT.Copy).then_inc(s_qs, 1)
                    if 0 <= c < NC:
                        rms(c, img, s_ss, s_ln, s_inv, s_xn, L_XS0)
                    if c + 2 < NC:
                        if c + 2 >= 1:
                            act.wait_ge(s_sqs, img * NC + c + 2)
                        for k in range(KT):
                            act.activation(SQ[:, k, :], X[:, k, (c + 2) * C:(c + 3) * C], ACT.Square, scale=RS[:, k:k + 1],
                                           bias=NBI[:, k:k + 1]).then_inc(s_sq, 1)
                    if 0 <= c - 1 < NC:
                        act.wait_ge(s_xn, img * NC + c)
                        act.activation(XN[:, 0, :, (c - 1) * C:c * C], HB[:, (c - 1) % 3, :, :], ACT.Copy).then_inc(s_hi, 1)
                for h in range(2):
                    act.wait_ge(s_kb, img + 1)
                    kh = KBUF[:, h * HALF:(h + 1) * HALF]
                    act.activation(kh, kh, ACT.Exp, scale=KSC[:, 0:1], bias=KB[:, 1:2], accum_out=SK[:, h:h + 1]).then_inc(s_ke, 1)
                for c in range(NC + 2):
                    if c < NC:
                        act.wait_ge(s_y, img * NC + c + 1)
                        if c >= 3:
                            act.wait_ge(s_x1, img * NC + c - 2)
                        for k in range(KT):
                            act.activation(HB[:, c % 3, k, :], PS[:, 2 + 2 * (c % 2) + k, :], ACT.Identity,
                                           scale=VEC[:, 2, k:k + 1], bias=VEC[:, 9, k:k + 1]).then_inc(s_yb, 1)
                        if c >= 1:
                            act.wait_ge(s_ysqs, img * NC + c)
                        for k in range(KT):
                            act.activation(SQ[:, k, :], PS[:, 2 + 2 * (c % 2) + k, :], ACT.Square,
                                           bias=VEC[:, 1, k:k + 1]).then_inc(s_ysq, 1)
                    if 0 <= c - 1 < NC:
                        rms(c - 1, img, s_yss, s_yln, s_yinv, s_yn, L_RMS)
                rstd(img * 2 + 2)
                for c in range(NC):
                    act.wait_ge(s_h1, img * 2 * NC + 2 * c + 2)
                    act.activation(XN[:, 0, :, c * C:(c + 1) * C], HB[:, c % 3, :, :], ACT.Copy).then_inc(s_hi1, 1)
                with act.Fori(0, PAIRS) as pair:
                    pp = img * PAIRS + pair
                    act.wait_ge(s_pad, (img + 1) * TY * RB * 3)
                    for n in range(TY * NC):
                        ty, t, bh = n // NC, n % RB, n % NC // RB
                        act.wait_ge(s_pj, pp * TY * NC + n + 2)
                        act.activation(padded(ty, 0, HB8 * bh, HB8, t), PS[:, n % 4, :].rearrange("p (b w) -> p b w", w=W),
                                       ACT.Copy, scale=PROJ).then_inc(s_phi, 1)
                    for u in range(DU):
                        act.wait_ge(s_dt, pp * DU + u + 1)
                        if u >= 2:
                            act.wait_ge(s_dkv, pp * DU + u - 1)
                        act.activation(KTb[0:TP, u % 2, :, :].rearrange("p j m -> p (j m)"), PS[0:TP, 4, :], ACT.Relu,
                                       scale=MX[0:TP, 1, 1:2]).then_inc(s_dk, 1)
                    for n in range(SLOTS):
                        for what, q, h in slot_steps(n):
                            i = pp * 2 * QUADS + 2 * q + h
                            if what == "trans":
                                act.wait_ge(s_at, i + 1)
                                if 2 * q + h >= 2:
                                    act.wait_ge(s_akv, i - 1)
                                act.activation(KTb[:, h, :, :].rearrange("p j m -> p (j m)"), PS[:, 4, :], ACT.Copy).then_inc(s_ak, 1)
                            if what == "den":
                                act.wait_ge(s_den, i + 1)
                                if q >= 1:
                                    act.wait_ge(s_qd, i - 1)
                                act.activation(DN[:, h, :], PS[:, 7, :], ACT.Ln, bias=const(E_DEN)).then_inc(s_dln, 1)
                                act.wait_ge(s_dln, i + 1)
                                act.activation(DN[:, h, :], DN[:, h, :], ACT.Exp, scale=-1.0).then_inc(s_dex, 1)
                        for what, q, h in slot_steps(n):
                            if what == "den" and h == 1:
                                act.wait_ge(s_qd, pp * 2 * QUADS + 2 * q + 2)
                                act.dma_start(QA[32 * q:32 * q + 32, :, :], OQ[:, q % 2, :]).then_inc(s_qa[q % 2], 16)
                        if n < CONVS and n % TY != 1:
                            q, ty = n // TY, n % TY
                            act.wait_ge(s_conv, pp * CONVS + n + 3)
                            if ty == 0 and q >= 1:
                                act.wait_ge(s_at, pp * 2 * QUADS + 2 * q)
                            if ty == 2 and q >= 2:
                                act.wait_ge(s_qa[q % 2], (pp * (QUADS // 2) + q // 2) * 16)
                            act.activation((OK[:, :] if ty == 0 else OQ[:, q % 2, :]).rearrange("p (a b) -> p a b", a=2),
                                           PS[:, 2 * (n % 2):2 * (n % 2) + 2, :], ACT.Relu, scale=SCA[:, 0:1]).then_inc(s_ev[ty], 1)
                    for c in range(NC):
                        act.wait_ge(s_fd, pp * NC + c + 1)
                        if c >= 2:
                            act.wait_ge(s_fq, pp * NC + c - 1)
                        act.activation(DN[:, c % 2, :], PS[:, 4 + c % 2, :], ACT.Ln, bias=const(E_DEN)).then_inc(s_fln, 1)
                        act.wait_ge(s_fln, pp * NC + c + 1)
                        act.activation(DN[:, c % 2, :], DN[:, c % 2, :], ACT.Exp, scale=-1.0).then_inc(s_fex, 1)

        @block.vector
        def _(dve):
            V = nc.vector
            chain = [0]

            def link(ins):
                chain[0] += 1
                ins.then_inc(s_setg, 1)
                dve.wait_ge(s_setg, chain[0])

            dve.sem_inc(s_pj, 1)
            dve.sem_inc(s_conv, 2)
            dve.sem_inc(s_p, 2)
            dve.sem_inc(s_fin, 1)
            dve.wait_ge(s_load, 16 * 8)
            for k in range(KT):
                link(V.tensor_scalar(W0F[:, k, :], W0F[:, k, :], VEC[:, 0, k:k + 1], CH ** 0.5, ALU.mult, ALU.mult))
            for j, a in enumerate((W0F, W1F, PW, DW)):
                link(V.tensor_reduce(MX[:, 0, j:j + 1], a if j > 1 else a.rearrange("p k n -> p (k n)"), AX, ALU.max,
                                     apply_absolute_value=True))
            V.tensor_scalar(SK[:, 0:1], MX[:, 0, 0:1], 1.0, None, ALU.mult).then_inc(s_set, 1)
            dve.wait_ge(s_allmax, 1)
            link(V.tensor_scalar(MX[:, 1, :], MX[:, 1, :], 1e-30, None, ALU.max))
            link(V.reciprocal(MX[:, 2, :], MX[:, 1, :]))
            link(V.tensor_scalar(KSC[:, :], MX[:, 1, 0:1], 1.0 / (WS * XS0), None, ALU.mult))
            link(V.tensor_tensor(SCA[:, :], MX[:, 1, 1:2], MX[:, 1, 2:3], ALU.mult))
            link(V.tensor_scalar(SCA[:, :], SCA[:, :], MX[:, 1, 3:4], 1.0 / WS, ALU.mult, ALU.mult))
            link(V.tensor_scalar(PW, PW, MX[:, 2, 2:3], WS, ALU.mult, ALU.mult))
            link(V.tensor_scalar(DW, DW, MX[:, 2, 3:4], None, ALU.mult))
            link(V.tensor_scalar(W0F, W0F, MX[:, 2, 0:1], WS, ALU.mult, ALU.mult))
            link(V.tensor_copy(W0[:, 0, :, :], W0F))
            link(V.tensor_tensor(W0[:, 1, :, :], W0F, W0[:, 0, :, :], ALU.subtract))
            link(V.tensor_scalar(W1F, W1F, MX[:, 2, 1:2], WS, ALU.mult, ALU.mult))
            for q in range(PAIRS):
                part = W1F[:, :, q * TY * P:(q + 1) * TY * P]
                link(V.tensor_copy(W1S[:, q, 0, :, :], part))
                V.tensor_tensor(W1S[:, q, 1, :, :], part, W1S[:, q, 0, :, :], ALU.subtract).then_inc(s_w1f, 1)
            dve.wait_ge(s_seta, 3)
            link(V.tensor_tensor(VEC[:, 7, :], VEC[:, 7, :], VEC[:, 3, :], ALU.mult))
            link(V.tensor_tensor(VEC[:, 9, :], VEC[:, 1, :], VEC[:, 2, :], ALU.mult))
            link(V.tensor_tensor(VEC[:, 8, :], VEC[:, 5, :], VEC[:, 7, :], ALU.mult))
            link(V.tensor_tensor(VEC[:, 8, :], VEC[:, 4, :], VEC[:, 8, :], ALU.subtract))
            pwv = PW.rearrange("p (g x o t) -> p g x o t", o=8, x=1, t=1)
            dwv = DW.rearrange("p (g x o t) -> p g x o t", x=TAPS, o=1, t=RB)
            for n in range(PAIRS * CONVS):
                for g in range(4):
                    if n >= 2:
                        dve.wait_ge(s_low, n - 1)
                    V.tensor_tensor(TF[:, n % 2, g, :].rearrange("p (x o t) -> p x o t", x=TAPS, t=RB),
                                    bc(pwv[:, 4 * n + g], [P, TAPS, 8, RB]), bc(dwv[:, 4 * n + g], [P, TAPS, 8, RB]),
                                    ALU.mult).then_inc(s_tw, 1)
                dve.wait_ge(s_hiw, n + 1)
                V.tensor_tensor(CW[:, n % 2, :, 1, :, :].rearrange("p g x m -> p g (x m)"), TF[:, n % 2, :, :],
                                CW[:, n % 2, :, 0, :, :].rearrange("p g x m -> p g (x m)"), ALU.subtract).then_inc(s_low, 1)

            def stats(c):
                for k in range(KT):
                    V.bn_stats(ST[:, k, c, :], X[:, k, c * C:(c + 1) * C]).then_inc(s_bn, 1)

            DCH = 2 * 7

            def norm(img, which, scale):
                at = [img * DCH + 7 * which]

                def step(ins):
                    at[0] = at[0] + 1
                    ins.then_inc(s_dchain, 1)
                    dve.wait_ge(s_dchain, at[0])

                count = img * 2 + which + 1
                gate(dve, s_bn, count * KT * NC)
                V.bn_aggr(MV[:, 0, :], ST[:, 0, :, :].rearrange("p a b -> p (a b)")).then_inc(s_dchain, 1)
                at[0] = at[0] + 1
                step(V.bn_aggr(MV[:, 1, :], ST[:, 1, :, :].rearrange("p a b -> p (a b)")))
                step(V.tensor_copy(G4[:, 0, :], MV[:, :, 0]))
                step(V.tensor_tensor(G4[:, 1, :], MV[:, :, 0], MV[:, :, 0], ALU.mult))
                V.tensor_tensor(G4[:, 1, :], MV[:, :, 1], G4[:, 1, :], ALU.add).then_inc(s_gin, 1)
                dve.wait_ge(s_gavg, count)
                step(V.tensor_copy(G4[:, 0:2, :], PS[:, 7, 0:4].rearrange("p (a b) -> p a b", a=2)))
                step(V.tensor_tensor(G4[:, 2, :], G4[:, 0, :], G4[:, 0, :], ALU.mult))
                V.tensor_tensor(G4[:, 2, :], G4[:, 1, :], G4[:, 2, :], ALU.subtract).then_inc(s_gvar, 1)
                dve.wait_ge(s_grs, count)
                step(V.tensor_scalar(RS[:, :], RS[:, :], scale, None, ALU.mult))
                V.scalar_tensor_tensor(out=NBI[:, :], in0=G4[:, 0, :], scalar=-1.0, in1=RS[:, :], op0=ALU.mult,
                                       op1=ALU.mult).then_inc(s_gn, 1)

            with dve.Fori(0, IMAGES) as img:
                for h in range(2):
                    dve.wait_ge(s_x[h], img * 16 + 16)
                    for c in range(h * NC // 2, (h + 1) * NC // 2):
                        stats(c)
                norm(img, 0, 1.0)
                for c in range(NC + 5):
                    d = c - 3
                    if 0 <= d < NC:
                        dve.wait_ge(s_kp, img * NC + d + 1)
                        V.tensor_reduce(KMX[:, d:d + 1], PS[:, 2 + d % 2, :], AX, ALU.max).then_inc(s_kmx, 1)
                        qv = PS[:, 4, :].rearrange("p (j h d) -> p j h d", j=4, d=D0)
                        dve.wait_ge(s_qp, img * NC + d + 1)
                        V.tensor_reduce(QX[:, d % 2, :, :], qv, AX, ALU.max).then_inc(s_qmx, 1)
                        dve.wait_ge(s_qmx, img * NC + d + 1)
                        if d >= 2:
                            dve.wait_ge(s_qt, img * NC + d - 1)
                        V.tensor_tensor(QM[:, d % 2, :].rearrange("p (j h d) -> p j h d", j=4, d=D0), qv,
                                        bc(QX[:, d % 2, :, :].rearrange("p j (h o) -> p j h o", o=1), [P, 4, HEADS0, D0]),
                                        ALU.subtract).then_inc(s_qsub, 1)
                    d = c - 4
                    if 0 <= d < NC:
                        qm = QM[:, d % 2, :].rearrange("p (j h d) -> p j h d", j=4, d=D0)
                        dve.wait_ge(s_qe, img * NC + d + 1)
                        V.tensor_reduce(QSM[:, d % 2, :, :], qm, AX, ALU.add).then_inc(s_qsum, 1)
                        dve.wait_ge(s_qsum, img * NC + d + 1)
                        V.reciprocal(QR[:, d % 2, :, :], QSM[:, d % 2, :, :]).then_inc(s_qr, 1)
                        dve.wait_ge(s_qr, img * NC + d + 1)
                        V.tensor_tensor(qm, qm, bc(QR[:, d % 2, :, :].rearrange("p j (h o) -> p j h o", o=1), [P, 4, HEADS0, D0]),
                                        ALU.mult).then_inc(s_qn, 1)
                    if c < NC:
                        hb = HB[:, c % 3, :, :]
                        dve.wait_ge(s_h, img * 2 * NC + 2 * c + 2)
                        dve.wait_ge(s_inv, img * NC + c + 1)
                        V.tensor_tensor(hb, hb, bc(INV[:, c % 2:c % 2 + 1, :], [P, KT, C]), ALU.mult).then_inc(s_xn, 1)
                    if 1 <= c <= NC:
                        dve.wait_ge(s_hi, img * NC + c)
                        cols = slice((c - 1) * C, c * C)
                        V.tensor_tensor(XN[:, 1, :, cols], HB[:, (c - 1) % 3, :, :], XN[:, 0, :, cols], ALU.subtract).then_inc(s_lo, 1)
                dve.wait_ge(s_kmx, img * NC + NC)
                V.tensor_reduce(KB[:, 0:1], KMX[:, :], AX, ALU.max).then_inc(s_sk, 1)
                dve.wait_ge(s_sk, img * 3 + 1)
                dve.wait_ge(s_kc, img * NC + NC)
                V.scalar_tensor_tensor(out=KB[:, 1:2], in0=KB[:, 0:1], scalar=-1.0, in1=KSC[:, 0:1], op0=ALU.mult,
                                       op1=ALU.mult).then_inc(s_kb, 1)
                for d in range(NC):
                    dve.wait_ge(s_ket, img * NC + d + 1)
                    if d >= 2:
                        dve.wait_ge(s_ctx, img * NC + d - 1)
                    V.tensor_copy(EKT[:, d % 2, :, :].rearrange("p j m -> p (j m)"), PS[:, 2 + d % 2, :]).then_inc(s_ekt, 1)
                dve.wait_ge(s_ke, img * 2 + 2)
                V.tensor_tensor(SK[:, 2:3], SK[:, 0:1], SK[:, 1:2], ALU.add).then_inc(s_sk, 1)
                dve.wait_ge(s_sk, img * 3 + 2)
                V.reciprocal(SK[:, 3:4], SK[:, 2:3]).then_inc(s_sk, 1)
                dve.wait_ge(s_ctx, img * NC + NC)
                V.tensor_tensor(SM, PS[:, 7, 0:P], m32, ALU.mult).then_inc(s_sm, 1)
                dve.wait_ge(s_mp, img + 1)
                dve.wait_ge(s_sk, img * 3 + 3)
                V.tensor_scalar(MM, PS[:, 6, 0:CH], SK[:, 3:4], D0 ** -0.5, ALU.mult, ALU.mult).then_inc(s_mm, 1)
                for c in range(NC + 2):
                    if c < NC:
                        hb = HB[:, c % 3, :, :]
                        dve.wait_ge(s_yb, img * 2 * NC + 2 * c + 2)
                        dve.wait_ge(s_yinv, img * NC + c + 1)
                        V.tensor_tensor(hb, hb, bc(INV[:, c % 2:c % 2 + 1, :], [P, KT, C]), ALU.mult).then_inc(s_yn, 1)
                    if c >= 2:
                        dve.wait_ge(s_x1, img * NC + c - 1)
                        stats(c - 2)
                norm(img, 1, XS1)
                for c in range(NC):
                    dve.wait_ge(s_hi1, img * NC + c + 1)
                    cols = slice(c * C, (c + 1) * C)
                    V.tensor_tensor(XN[:, 1, :, cols], HB[:, c % 3, :, :], XN[:, 0, :, cols], ALU.subtract).then_inc(s_lo1, 1)
                with dve.Fori(0, PAIRS) as pair:
                    pp = img * PAIRS + pair
                    for n in range(TY * NC):
                        ty, t, bh = n // NC, n % RB, n % NC // RB
                        dve.wait_ge(s_phi, pp * TY * NC + n + 1)
                        V.scalar_tensor_tensor(out=padded(ty, 1, HB8 * bh, HB8, t),
                                               in0=PS[:, n % 4, :].rearrange("p (b w) -> p b w", w=W), scalar=PROJ,
                                               in1=padded(ty, 0, HB8 * bh, HB8, t), op0=ALU.mult,
                                               op1=ALU.subtract).then_inc(s_plo, 1)
                    for u in range(DU):
                        dve.wait_ge(s_dt, pp * DU + u + 1)
                        if u >= 2:
                            dve.wait_ge(s_dkv, pp * DU + u - 1)
                        V.tensor_scalar(VTb[0:TP, u % 2, :, 0:P], PS[0:TP, 5, :].rearrange("p (j m) -> p j m", j=4),
                                        MX[0:TP, 1, 1:2], None, ALU.mult).then_inc(s_dv, 1)
                    dve.wait_ge(s_dkv, pp * DU + DU)
                    V.tensor_tensor(KVM[:, :], PS[:, 7, 0:P], m8, ALU.mult).then_inc(s_dkm, 1)
                    V.tensor_copy(KS[:, 0:1], PS[:, 7, P:P + 1]).then_inc(s_dks, 1)
                    dve.wait_ge(s_dks, pp * 2 + 1)
                    V.tensor_scalar(DMD[:, :], m8, KS[:, 0:1], None, ALU.mult).then_inc(s_dks, 1)
                    dve.wait_ge(s_dtr, pp + 1)
                    V.tensor_copy(KVS[:, :], PS[:, 6, 0:P]).then_inc(s_dkm, 1)
                    dve.wait_ge(s_dp, pp + 1)
                    V.tensor_copy(PD[:, :], PS[:, 6, CH:2 * CH]).then_inc(s_pd, 1)
                    for n in range(SLOTS):
                        for what, q, h in slot_steps(n):
                            i = pp * 2 * QUADS + 2 * q + h
                            if what == "trans":
                                dve.wait_ge(s_at, i + 1)
                                if 2 * q + h >= 2:
                                    dve.wait_ge(s_akv, i - 1)
                                V.tensor_copy(VTb[:, h, :, 0:P], PS[:, 5, :].rearrange("p (j m) -> p j m", j=4)).then_inc(s_av, 1)
                            if what == "kv" and h == 1:
                                dve.wait_ge(s_akv, i + 1)
                                V.tensor_tensor(KVM[:, :], PS[:, 6, 0:P], mgt, ALU.mult).then_inc(s_kvm, 1)
                                V.tensor_copy(KS[:, 0:1], PS[:, 6, P:P + 1]).then_inc(s_kvm, 1)
                            if what == "sel":
                                j = pp * QUADS + q
                                dve.wait_ge(s_sel, j + 1)
                                V.tensor_copy(KVS[:, 0:32], PS[:, 6, CH:CH + 32]).then_inc(s_kvs, 1)
                                V.tensor_copy(KS[:, 1:2], PS[:, 6, CH + 32:CH + 33]).then_inc(s_kvs, 1)
                                dve.wait_ge(s_kvs, j * 3 + 2)
                                if q >= 1:
                                    dve.wait_ge(s_den, pp * 2 * QUADS + 2 * q)
                                V.tensor_scalar(DM[:, :], mgt, KS[:, 1:2], None, ALU.mult).then_inc(s_kvs, 1)
                            if what == "p":
                                dve.wait_ge(s_p, pp * QUADS + q + 3)
                                V.tensor_copy(PA[32 * q:32 * q + 32, :], PS[32 * q:32 * q + 32, 6, CH:2 * CH]).then_inc(s_pa, 1)
                        if n < CONVS and n % TY == 1:
                            q = n // TY
                            dve.wait_ge(s_conv, pp * CONVS + n + 3)
                            if q >= 1:
                                dve.wait_ge(s_at, pp * 2 * QUADS + 2 * q)
                            V.tensor_scalar(OV[:, :].rearrange("p (a b) -> p a b", a=2), PS[:, 2 * (n % 2):2 * (n % 2) + 2, :],
                                            SCA[:, 0:1], None, ALU.mult).then_inc(s_ev[1], 1)
                    for c in range(NC + 2):
                        if c < NC:
                            dve.wait_ge(s_qf, pp * NC + c + 1)
                            V.tensor_scalar(QF[:, c % 2, :], QF[:, c % 2, :], 0.0, MX[:, 1, 1:2], ALU.max, ALU.mult).then_inc(s_qrl, 1)
                        d = c - 1
                        if 0 <= d < NC:
                            dve.wait_ge(s_fex, pp * NC + d + 1)
                            if d >= 2:
                                dve.wait_ge(s_fo, pp * NC + d - 1)
                            V.tensor_tensor(QN[:, d % 2, :], QF[:, d % 2, :], DN[:, d % 2, :], ALU.mult).then_inc(s_fq, 1)
                        d = c - 2
                        if d >= 0:
                            t, bh = d % RB, d // RB
                            dve.wait_ge(s_fo, pp * NC + d + 1)
                            dve.wait_ge(s_bias, (img + 1) * KT)
                            for k in range(KT):
                                xs = rows(X[:, k, :], HB8 * bh, HB8, t)
                                V.scalar_tensor_tensor(out=xs, in0=PS[:, 2 * (d % 2) + k, :].rearrange("p (b w) -> p b w", w=W),
                                                       scalar=VEC[:, 7, k:k + 1], in1=xs, op0=ALU.mult, op1=ALU.add).then_inc(s_fin, 1)

        @block.tensor
        def _(pe):
            MM_ = nc.tensor.matmul
            SPLIT = ((0, 0), (1, 0), (0, 1))

            def gavg(count):
                pe.wait_ge(s_gin, count)
                MM_(PS[:, 7, 0:4], g8, G4[:, 0:2, :].rearrange("p a b -> p (a b)"), start=True, stop=True).then_inc(s_gavg, 1)

            def total(img, c, ready, signal, used):
                pe.wait_ge(ready, img * NC + c + 1)
                if c >= 2:
                    pe.wait_ge(used, img * NC + c - 1)
                MM_(PS[:, c % 2, :], ones, SQS[:, c % 2, :], start=True, stop=True).then_inc(signal, 1)

            def turn_q(img, d):
                pe.wait_ge(s_qn, img * NC + d + 1)
                if d >= 1:
                    pe.wait_ge(s_qs, img * NC + d)
                for j in range(4):
                    last = nc.tensor.transpose(PS[:, 6, j * P:(j + 1) * P], QM[:, d % 2, j * P:(j + 1) * P], ident)
                last.then_inc(s_qt, 1)

            pe.wait_ge(s_load, 16 * 8)
            pe.wait_ge(s_seta, 3)
            pe.wait_ge(s_one, 1)
            with pe.Fori(0, IMAGES) as img:
                gavg(img * 2 + 1)
                for c in range(-1, NC + 5):
                    if 0 <= c - 5 < NC:
                        turn_q(img, c - 5)
                    if c + 1 < NC:
                        total(img, c + 1, s_sqs, s_ss, s_ln)
                    d = c - 2
                    if not 0 <= d < NC:
                        continue
                    pe.wait_ge(s_lo, img * NC + d + 1)
                    if d >= 2:
                        pe.wait_ge(s_kmx, img * NC + d - 1)
                        pe.wait_ge(s_kc, img * NC + d - 1)
                    i = 0
                    for k in range(KT):
                        for a, b in SPLIT:
                            last = MM_(PS[:, 2 + d % 2, :], W0[:, a, k, HID:2 * HID], XN[:, b, k, d * C:(d + 1) * C],
                                       start=(i == 0), stop=(i == 3 * KT - 1))
                            i += 1
                    last.then_inc(s_kp, 1)
                    for bank, o, free, signal in ((5, 2 * HID, s_vc, s_vp), (4, 0, s_qsub, s_qp)):
                        if d >= 1:
                            pe.wait_ge(free, img * NC + d)
                        for j in range(4):
                            at = d * C + j * P
                            i = 0
                            for k in range(KT):
                                for a, b in SPLIT:
                                    last = MM_(PS[:, bank, j * P:(j + 1) * P], XN[:, b, k, at:at + P], W0[:, a, k, o:o + HID],
                                               start=(i == 0), stop=(i == 3 * KT - 1))
                                    i += 1
                        last.then_inc(signal, 1)

                def turn_k(d):
                    pe.wait_ge(s_ke, img * 2 + 1 + d // (NC // 2))
                    if d >= 2:
                        pe.wait_ge(s_ekt, img * NC + d - 1)
                    for j in range(4):
                        at = d * C + j * P
                        last = nc.tensor.transpose(PS[:, 2 + d % 2, j * P:(j + 1) * P], KBUF[:, at:at + P], ident)
                    last.then_inc(s_ket, 1)

                turn_k(0)
                for d in range(NC):
                    if d + 1 < NC:
                        turn_k(d + 1)
                    pe.wait_ge(s_ekt, img * NC + d + 1)
                    for j in range(4):
                        at = d * C + j * P
                        last = MM_(PS[:, 7, 0:P], VT[:, at:at + P], EKT[:, d % 2, j, :], start=(d == 0 and j == 0),
                                   stop=(d == NC - 1 and j == 3))
                    last.then_inc(s_ctx, 1)
                pe.wait_ge(s_sm, img + 1)
                pe.wait_ge(s_qs, img * NC + NC)
                MM_(PS[:, 6, 0:CH], SM, WOUT[:, :], start=True, stop=True).then_inc(s_mp, 1)
                pe.wait_ge(s_mm, img + 1)
                for c in range(NC + 1):
                    if c < NC:
                        if c >= 2:
                            pe.wait_ge(s_ysq, img * 2 * NC + 2 * c - 2)
                        for k in range(KT):
                            last = MM_(PS[:, 2 + 2 * (c % 2) + k, :], MM[:, k * P:(k + 1) * P], QS[:, c * C:(c + 1) * C],
                                       start=True, stop=True)
                        last.then_inc(s_y, 1)
                    if c >= 1:
                        total(img, c - 1, s_ysqs, s_yss, s_yln)
                gavg(img * 2 + 2)
                with pe.Fori(0, PAIRS) as pair:
                    pp = img * PAIRS + pair
                    pe.wait_ge(s_w1, pp * 16 + 16)
                    pe.wait_ge(s_fin, pp * 2 * NC + 1)
                    for n in range(TY * NC):
                        ty, t, bh = n // NC, n % RB, n % NC // RB
                        if n in (0, RB):
                            pe.wait_ge(s_lo1, img * NC + (n // RB + 1) * NC // 2)
                        if n >= 4:
                            pe.wait_ge(s_plo, pp * TY * NC + n - 3)
                        i = 0
                        for k in range(KT):
                            for a, b in SPLIT:
                                last = MM_(PS[:, n % 4, :].rearrange("p (b w) -> p b w", w=W), W1[:, a, k, ty, :],
                                           rows(XN[:, b, k, :], HB8 * bh, HB8, t), start=(i == 0), stop=(i == 3 * KT - 1))
                                i += 1
                        last.then_inc(s_pj, 1)
                    for u in range(DU + 1):
                        if u < DU:
                            if u == 0:
                                pe.wait_ge(s_plo, pp * TY * NC + 2 * NC)
                            else:
                                pe.wait_ge(s_dk, pp * DU + u)
                                pe.wait_ge(s_dv, pp * DU + u)
                            for ty in range(2):
                                for j in range(4):
                                    for a in range(2):
                                        last = MM_(PS[0:TP, 4 + ty, j * P:(j + 1) * P], stretch(ty, a, 4 * u + j), I16[:, :],
                                                   start=(a == 0), stop=(a == 1))
                            last.then_inc(s_dt, 1)
                        v = u - 1
                        if v >= 0:
                            pe.wait_ge(s_dk, pp * DU + v + 1)
                            pe.wait_ge(s_dv, pp * DU + v + 1)
                            for j in range(4):
                                last = MM_(PS[:, 7, 0:P + 1], KTb[0:TP, v % 2, j, :], VTb[0:TP, v % 2, j, :],
                                           start=(v == 0 and j == 0), stop=(v == DU - 1 and j == 3))
                            last.then_inc(s_dkv, 1)
                    pe.wait_ge(s_dkm, pp * 2 + 1)
                    MM_(PS[:, 6, 0:P], KVM[:, :], ident, start=True, stop=True).then_inc(s_dtr, 1)
                    pe.wait_ge(s_dkm, pp * 2 + 2)
                    nc.tensor.matmul(PS[:, 6, CH:2 * CH], KVS[:, :], WPD[:, pair, :], start=True, stop=True).then_inc(s_dp, 1)
                    for n in range(SLOTS):
                        for what, q, h in slot_steps(n):
                            i = pp * 2 * QUADS + 2 * q + h
                            j4 = pp * QUADS + q
                            if what == "trans":
                                pe.wait_ge(s_ev[0], j4 + 1)
                                pe.wait_ge(s_ev[1], j4 + 1)
                                if 2 * q + h >= 1:
                                    pe.wait_ge(s_ak, i)
                                    pe.wait_ge(s_av, i)
                                for src, bank in ((OK, 4), (OV, 5)):
                                    for j in range(4):
                                        at = h * C + j * P
                                        last = nc.tensor.transpose(PS[:, bank, j * P:(j + 1) * P], src[:, at:at + P], ident)
                                last.then_inc(s_at, 1)
                            if what == "kv":
                                pe.wait_ge(s_ak, i + 1)
                                pe.wait_ge(s_av, i + 1)
                                if h == 0:
                                    if q >= 1:
                                        pe.wait_ge(s_pa, j4)
                                    else:
                                        pe.wait_ge(s_pd, pp + 1)
                                for j in range(4):
                                    last = MM_(PS[:, 6, 0:P + 1], KTb[:, h, j, :], VTb[:, h, j, :],
                                               start=(h == 0 and j == 0), stop=(h == 1 and j == 3))
                                last.then_inc(s_akv, 1)
                            if what == "sel":
                                pe.wait_ge(s_kvm, j4 * 2 + 2)
                                MM_(PS[:, 6, CH:CH + 32], KVM[:, :], sel, start=True, stop=True)
                                MM_(PS[:, 6, CH + 32:CH + 33], tsum, KS[:, 0:1], start=True, stop=True).then_inc(s_sel, 1)
                            if what == "p":
                                pe.wait_ge(s_kvs, j4 * 3 + 3)
                                pe.wait_ge(s_wpa[q % 2], (pp * (QUADS // 2) + q // 2 + 1) * 16)
                                MM_(PS[32 * q:32 * q + 32, 6, CH:2 * CH], KVS[:, 0:32], WPA[:, q % 2, :], start=True,
                                    stop=True).then_inc(s_p, 1)
                            if what == "den":
                                pe.wait_ge(s_ev[2], j4 + 1)
                                if 2 * q + h >= 1:
                                    pe.wait_ge(s_dln, i)
                                MM_(PS[:, 7, :], DM[:, :], OQ[:, q % 2, h * C:(h + 1) * C], start=True, stop=True).then_inc(s_den, 1)
                        if n < CONVS:
                            m = n % 2
                            q, ty = n // TY, n % TY
                            uses = CONVS // 2
                            pe.wait_ge(s_cw[m], (pp * uses + n // 2 + 1) * 16)
                            pe.wait_ge(s_ct[m], (pp * uses + n // 2 + 1) * 128)
                            if n >= 2:
                                pq, pt = (n - 2) // TY, (n - 2) % TY
                                pe.wait_ge(s_ev[pt], pp * QUADS + pq + 1)
                            for ch in range(2):
                                i = 0
                                for a in range(2):
                                    for dx in range(TAPS):
                                        for g in range(4):
                                            mv = CT[:, m, g, :].rearrange("p (b w) -> p b w", w=WP)[:, ch * HB8:(ch + 1) * HB8, dx:dx + W]
                                            last = MM_(PS[32 * g:32 * g + 32, 2 * m + ch, :].rearrange("p (b w) -> p b w", w=W),
                                                       CW[:, m, g, a, dx, :], mv, start=(i == 0), stop=(i == 2 * TAPS - 1))
                                        i += 1
                            last.then_inc(s_conv, 1)
                    for c in range(NC + 1):
                        if c < NC:
                            pe.wait_ge(s_qrl, pp * NC + c + 1)
                            if c >= 2:
                                pe.wait_ge(s_fln, pp * NC + c - 1)
                            MM_(PS[:, 4 + c % 2, :], DMD[:, :], QF[:, c % 2, :], start=True, stop=True).then_inc(s_fd, 1)
                        d = c - 1
                        if d >= 0:
                            t, bh = d % RB, d // RB
                            pe.wait_ge(s_fq, pp * NC + d + 1)
                            if d == 0:
                                for m in range(2):
                                    pe.wait_ge(s_qa[m], (pp + 1) * (QUADS // 2) * 16)
                                pe.wait_ge(s_pa, (pp + 1) * QUADS)
                            if d >= 2:
                                pe.wait_ge(s_fin, pp * 2 * NC + 2 * (d - 1) + 1)
                            for k in range(KT):
                                MM_(PS[:, 2 * (d % 2) + k, :], PD[:, k * P:(k + 1) * P], QN[:, d % 2, :], start=True, stop=False)
                                last = MM_(PS[:, 2 * (d % 2) + k, :], PA[:, k * P:(k + 1) * P], QA[:, t, bh * C:(bh + 1) * C],
                                           start=False, stop=True)
                            last.then_inc(s_fo, 1)


def kernel(x, L0_conv_W_qkv, L0_conv_W_out, L0_conv_b_out, L0_conv_g_norm, L0_conv_g_out, L1_conv_w_qkv,
           L1_conv_w_dw, L1_conv_w_pw, L1_conv_w_proj, L1_conv_bn_gamma, L1_conv_bn_beta, L1_conv_bn_mean,
           L1_conv_bn_var):
    import concourse.bacc as bacc
    from concourse.bass_utils import run_bass_kernel_spmd

    kind = [1, 2, 0]
    heads = 4 * QUADS
    by_tile = np.array([[[3 * (p * heads + h) + kind[ty] for h in range(heads)] for ty in range(TY)]
                        for p in range(PAIRS)])
    by_conv = by_tile.reshape(PAIRS, TY, QUADS, 4).transpose(0, 2, 1, 3).reshape(-1)
    w1 = np.asarray(L1_conv_w_qkv).reshape(96, 8, CH)[by_tile.reshape(-1)].reshape(768, CH)
    pw = np.asarray(L1_conv_w_pw)[by_conv]
    pwp = np.broadcast_to(pw.transpose(2, 0, 1)[None, :, None, None], (2, 8, 2, 4, 96, 8)).reshape(P, -1)
    dw = np.asarray(L1_conv_w_dw).reshape(96, 8, TAPS, TAPS)[by_conv]
    dwp = np.zeros((2, 8, 2, 4, 96, TAPS, RB), np.float32)
    for half in range(2):
        for t in range(4):
            for row in range(RB):
                dy = 4 * half + t - row
                if 0 <= dy < TAPS:
                    dwp[half, :, :, t, :, :, row] = dw[:, :, dy, :].transpose(1, 0, 2)[:, None]
    wp = np.asarray(L1_conv_w_proj).T.reshape(2, PAIRS, P, CH)
    wpa = np.repeat(wp[1].reshape(PAIRS * QUADS, 32, 1, CH), RB, axis=2).reshape(PAIRS * QUADS, P, CH)
    vecs = np.stack([np.asarray(v).reshape(KT, P).T for v in (
        L0_conv_g_norm, L0_conv_b_out, L0_conv_g_out, L1_conv_bn_gamma, L1_conv_bn_beta, L1_conv_bn_mean,
        L1_conv_bn_var)], axis=1)
    arrays = {
        "x": np.asarray(x).reshape(IMAGES, CH, N), "cst": constants(),
        "w0t": np.asarray(L0_conv_W_qkv).T, "vecs": vecs,
        "woutt": np.asarray(L0_conv_W_out).T, "w1t": w1.T, "pwp": pwp, "dwp": dwp.reshape(P, -1), "wpd": wp[0],
        "wpa": wpa,
    }
    nc = bacc.Bacc("TRN2", target_bir_lowering=False, num_devices=1)
    args, given = [], {}
    for name, a in arrays.items():
        a = np.ascontiguousarray(a)
        given["in_" + name] = a
        args.append(nc.dram_tensor("in_" + name, a.shape, mybir.dt.from_np(a.dtype), kind="ExternalInput").ap())
    args.append(nc.dram_tensor("out_y", (IMAGES, CH, N), F32, kind="ExternalOutput").ap())
    two_layers(nc, *args)
    r = run_bass_kernel_spmd(nc, [given], core_ids=[0])
    return r.results[0]["out_y"].reshape(IMAGES, CH, H, W)
```

```python
from contextlib import ExitStack
import math

import numpy as np
import concourse.bass as bass
from concourse import mybir

F32, F16 = mybir.dt.float32, mybir.dt.float16
ALU, ACT = mybir.AluOpType, mybir.ActivationFunctionType
AX = mybir.AxisListType.X
RMAX = bass.bass_isa.ReduceOp.max

IMAGES, CH, H, W = 16, 256, 64, 64
N = H * W
P = 128
KT = CH // P
C = 512
NC = N // C
HALF = N // 2
TP = 124
DU = 9
HEADS0, D0 = 4, 32
HID = HEADS0 * D0
D1 = 8
PAIRS = 2
QUADS = 4
TY = 3
TAPS = 5
RB = 4
EK = 4
NH = 4
NB = H // RB
WP = W + TAPS - 1
GCOL = TAPS * D1 * RB
CONVS = QUADS * TY
SLOTS = CONVS + 2 * TY
WS = 1024.0
XS0, XS1 = 1024.0, 64.0
PROJ = 1.0 / (WS * XS1)

CI, CONE, CG8, CM32, CM8, CMGT, CTS, CSEL = (128 * j for j in range(8))
CSC = CSEL + 32
E_RMS, E_DEN, E_GN, L_XS0, L_RMS, CNUM = range(6)


def constants():
    a = np.zeros((P, CSC + CNUM), np.float32)
    r = np.arange(P)
    a[:, CI:CI + P] = r[:, None] == r
    a[:, CONE:CONE + P] = 1.0
    a[:, CG8:CG8 + P] = (r[:, None] // 8 == r // 8) / 8.0
    a[:, CM32:CM32 + P] = r[:, None] // D0 == r // D0
    a[:, CM8:CM8 + P] = r[:, None] // D1 == r // D1
    head, row, chan = r // 32, r % RB, r // RB
    a[:, CMGT:CMGT + P] = (head[:, None] == head) & (row[:, None] == row)
    a[:, CTS:CTS + P] = chan[:, None] == chan
    a[:, CSEL:CSEL + 32] = chan[:, None] == np.arange(32)
    a[:, CSC:] = [1e-12, 1e-15, 1e-5, math.log(XS0), math.log(CH ** 0.5)]
    return a




def bc(ap, shape):
    return ap.broadcast_to(shape)


def two_layers(nc, x, cst, w0t, vecs, woutt, w1t, pwp, dwp, wpd, wpa, out):
    ctx = ExitStack()
    with ctx:
        def sb(name, shape, dt=F32):
            return ctx.enter_context(nc.sbuf_tensor(name, shape, dt))

        def sem(name):
            return ctx.enter_context(nc.semaphore(name))

        w1_d = nc.dram_tensor("w1_split", (PAIRS, P, 2 * KT * TY * P), F16, kind="Internal").ap()
        wc_d = nc.dram_tensor("wc_split", (PAIRS * CONVS, P, 4 * 2 * GCOL), F16, kind="Internal").ap()

        X = sb("X", [P, KT, N])
        XN = sb("XN", [P, NC, 2, KT, C], F16)
        QKV = sb("QKV", [P, TY, 2, RB, NB + 1, WP], F16)
        CT = sb("CT", [P, 2, 4, NB * WP], F16)
        CW = sb("CW", [P, 2, 4, 2, TAPS, 32], F16)
        OK = sb("OK", [P, 2 * C])
        OV = sb("OV", [P, 2 * C])
        OQ = sb("OQ", [P, 2, 2 * C])
        QA = sb("QA", [P, RB, 2 * C])
        KTb = sb("KTb", [P, 2, 4, P])
        VTb = sb("VTb", [P, 2, 4, P + 1])
        DN = sb("DN", [P, 2, C])
        W0 = sb("W0", [P, 2, KT, 3 * HID], F16)
        W1 = sb("W1", [P, 2, KT, TY, P], F16)
        WOUT = sb("WOUT", [P, CH])
        WPD = sb("WPD", [P, PAIRS, CH])
        WPA = sb("WPA", [P, 2, CH])
        CO = sb("CO", [P, CSC + CNUM])
        I16 = sb("I16", [P, P], F16)
        PD = sb("PD", [P, CH])
        PA = sb("PA", [P, CH])
        KVM = sb("KVM", [P, P])
        KVS = sb("KVS", [P, P])
        DM = sb("DM", [P, P])
        DMD = sb("DMD", [P, P])
        KS = sb("KS", [P, 2])
        ST = sb("ST", [P, KT, NC, 6])
        MV = sb("MV", [P, KT, 2])
        G4 = sb("G4", [P, 4, 2])
        RS = sb("RS", [P, KT])
        NBI = sb("NBI", [P, KT])
        VEC = sb("VEC", [P, 10, KT])
        MX = sb("MX", [P, 3, 4])
        KSC = sb("KSC", [P, 1])
        SCA = sb("SCA", [P, 1])
        KMX = sb("KMX", [P, NC])
        KB = sb("KB", [P, 2])
        SK = sb("SK", [P, EK + 2])
        QX = sb("QX", [P, 2, 4, HEADS0])
        QSM = sb("QSM", [P, 2, 4, HEADS0])
        QR = sb("QR", [P, 2, 4, HEADS0])

        flat = QKV[:, :, :, :, :, :].rearrange("p a b c d e -> p (a b c d e)").bitcast(F32)
        KBUF, QS, VT = (flat[:, j * N:(j + 1) * N] for j in range(3))
        EKT = KTb
        ctf = CT[:, :, :, :].rearrange("p a b c -> p (a b c)").bitcast(F32)
        HB = ctf[:, 0:NH * KT * C].rearrange("p (s k n) -> p s k n", s=NH, k=KT)
        qaf = QA[:, :, :].rearrange("p a b -> p (a b)")
        SQ = OQ[:, :, :].rearrange("p s (k n) -> p s k n", k=KT)
        SQS = qaf[:, 2 * C:4 * C].rearrange("p (s n) -> p s n", s=2)
        INV = qaf[:, 4 * C:6 * C].rearrange("p (s n) -> p s n", s=2)
        QM = qaf[:, 6 * C:8 * C].rearrange("p (s n) -> p s n", s=2)
        MM = OV[:, 0:CH]
        SM = OV[:, CH:CH + P]
        QF, FD, QN = (ctf[:, a * C:b * C].rearrange("p (s n) -> p s n", n=C) for a, b in ((0, 3), (3, 5), (5, 7)))
        xf = XN[:, :, :, :, :].rearrange("p c a k n -> p (c a k n)")
        nw = KT * TY * 2 * P
        W0F = xf.bitcast(F32)[:, 0:KT * 3 * HID].rearrange("p (k n) -> p k n", k=KT)
        W1F = xf.bitcast(F32)[:, N:N + nw].rearrange("p (k n) -> p k n", k=KT)
        W1S = xf[:, N:N + 2 * nw].rearrange("p (q h k n) -> p q h k n", q=PAIRS, h=2, k=KT)
        RAW = xf.bitcast(F32).rearrange("p (c k n) -> p c k n", c=NC, k=KT)
        PW = flat[:, 0:96 * 8]
        DW = flat[:, 1024:1024 + 96 * 20]
        TF = flat[:, 4096:4096 + 2 * 4 * GCOL].rearrange("p (s g n) -> p s g n", s=2, g=4)

        PS = ctx.enter_context(nc.psum_tensor("PS", [P, 8, C], F32))

        ident, ones, g8 = CO[:, CI:CI + P], CO[:, CONE:CONE + P], CO[:, CG8:CG8 + P]
        m32, m8, mgt = CO[:, CM32:CM32 + P], CO[:, CM8:CM8 + P], CO[:, CMGT:CMGT + P]
        tsum, sel = CO[:, CTS:CTS + P], CO[:, CSEL:CSEL + 32]

        def const(j):
            return CO[:, CSC + j:CSC + j + 1]

        s_load = sem("s_load"); s_set = sem("s_set"); s_seta = sem("s_seta"); s_allmax = sem("s_allmax")
        s_hiw = sem("s_hiw"); s_tw = sem("s_tw"); s_low = sem("s_low"); s_wc = [sem(f"s_wc{j}") for j in range(2)]; s_w1s = sem("s_w1s")
        s_x = [sem(f"s_xin{h}") for h in range(2)]
        s_raw = [sem(f"s_raw{h}") for h in range(2)]
        s_out = [sem(f"s_out{h}") for h in range(2)]; s_w1f = sem("s_w1f")
        s_dchain = sem("s_dchain"); s_pchain = sem("s_pchain"); s_setg = sem("s_setg")
        s_bn = sem("s_bn"); s_gin = sem("s_gin"); s_gavg = sem("s_gavg"); s_gvar = sem("s_gvar")
        s_grs = sem("s_grs"); s_gn = sem("s_gn"); s_gln = sem("s_gln")
        s_h = sem("s_h"); s_sq = sem("s_sq"); s_sqs = sem("s_sqs"); s_ss = sem("s_ss"); s_ln = sem("s_ln")
        s_inv = sem("s_inv"); s_xn = sem("s_xn"); s_hi = sem("s_hi"); s_lo = sem("s_lo")
        s_kp = sem("s_kp"); s_vp = sem("s_vp"); s_qp = sem("s_qp")
        s_kmx = sem("s_kmx"); s_kc = sem("s_kc"); s_vc = sem("s_vc"); s_qmx = sem("s_qmx"); s_qsub = sem("s_qsub")
        s_qe = sem("s_qe"); s_qsum = sem("s_qsum"); s_qr = sem("s_qr"); s_qn = sem("s_qn"); s_qt = sem("s_qt"); s_qs = sem("s_qs")
        s_kb = sem("s_kb"); s_ke = sem("s_ke"); s_ket = sem("s_ket"); s_ekt = sem("s_ekt")
        s_ctx = sem("s_ctx"); s_sm = sem("s_sm"); s_mp = sem("s_mp"); s_mm = sem("s_mm"); s_sk = sem("s_sk")
        s_y = sem("s_y"); s_yb = sem("s_yb"); s_ysq = sem("s_ysq"); s_ysqs = sem("s_ysqs"); s_yss = sem("s_yss")
        s_yln = sem("s_yln"); s_yinv = sem("s_yinv"); s_yn = sem("s_yn"); s_x1 = sem("s_x1")
        s_pad = sem("s_pad"); s_hi1 = sem("s_hi1"); s_lo1 = sem("s_lo1"); s_h1 = sem("s_h1"); s_bias = sem("s_bias")
        s_w1 = sem("s_w1"); s_pj = sem("s_pj"); s_phi = sem("s_phi"); s_plo = sem("s_plo")
        s_dt = sem("s_dt"); s_dk = sem("s_dk"); s_dv = sem("s_dv"); s_dkv = sem("s_dkv")
        s_dkm = sem("s_dkm"); s_dtr = sem("s_dtr"); s_dks = sem("s_dks"); s_dp = sem("s_dp"); s_pd = sem("s_pd")
        s_cw = [sem(f"s_cw{j}") for j in range(2)]
        s_ct = [sem(f"s_ct{j}") for j in range(2)]
        s_conv = sem("s_conv"); s_ev = [sem(f"s_ev{j}") for j in range(TY)]
        s_at = sem("s_at"); s_ak = sem("s_ak"); s_av = sem("s_av"); s_akv = sem("s_akv"); s_kvm = sem("s_kvm")
        s_sel = sem("s_sel"); s_kvs = sem("s_kvs"); s_p = sem("s_p"); s_pa = sem("s_pa"); s_wpa = [sem(f"s_wpa{j}") for j in range(2)]
        s_den = sem("s_den"); s_dln = sem("s_dln"); s_dex = sem("s_dex"); s_qd = sem("s_qd"); s_qa = [[sem(f"s_qa{h}{j}") for j in range(2)] for h in range(2)]
        s_qf = sem("s_qf"); s_qrl = sem("s_qrl"); s_fd = sem("s_fd"); s_fln = sem("s_fln"); s_fex = sem("s_fex")
        s_fq = sem("s_fq"); s_fo = sem("s_fo"); s_fin = sem("s_fin"); s_one = sem("s_one"); s_gate = sem("s_gate")

        x_v = x.rearrange("i (k p) n -> i p k n", p=P)
        out_v = out.rearrange("i (k p) n -> i p k n", p=P)

        block = ctx.enter_context(nc.Block())

        def gate(eng, semaphore, value):
            eng.wait_ge(semaphore, value)
            eng.sem_inc(s_gate, 1)

        def slot_steps(n):
            q = n // TY
            steps = {0: [("sel", q - 2, 0), ("trans", q - 1, 0)],
                     1: [("trans", q - 1, 1), ("den", q - 2, 0), ("p", q - 2, 0), ("kv", q - 1, 0)],
                     2: [("den", q - 2, 1), ("kv", q - 1, 1)]}[n % TY]
            steps = [s for s in steps if 0 <= s[1] < QUADS]
            if n == 1:
                steps += [("turn", 0, 0)]
            if n == 2:
                steps += [("weights", 0, 0)]
            if n == CONVS:
                steps += [("q", 0, 0), ("q", 0, 1), ("q", 0, 2)]
            if n == CONVS + 2:
                steps += [("fd", 0, 0), ("fd", 0, 1)]
            return steps

        def rows(ap, b0, nb, t):
            return ap.rearrange("p (b t w) -> p b t w", t=RB, w=W)[:, b0:b0 + nb, t, :]

        def unit(n):
            return n // RB % TY, n % RB, n // (RB * TY)

        def units_of(ty):
            return RB * TY + RB * (ty + 1)

        def half_rows(part, k, half, t):
            return XN[:, half * NC // 2:(half + 1) * NC // 2, part, k, :].rearrange(
                "p c (b t w) -> p c b t w", t=RB, w=W)[:, :, :, t, :]

        def padded(ty, part, b0, nb, t):
            return QKV[:, ty, part, (t + 2) % RB, b0 + (t + 2) // RB:b0 + (t + 2) // RB + nb, 2:2 + W]

        def stretch(ty, part, ci):
            t = ci // DU
            at = (WP + NB * WP - DU * TP if t < 2 else 0) + TP * (ci % DU)
            return QKV[:, ty, part, t, :, :].rearrange("p b w -> p (b w)")[:, at:at + TP]

        HB8 = C // W
        DBANK = (4, 0)
        VBANK = (5, 7)

        @block.sync
        def _(sp):
            ld = [(CO[:, :], cst), (W0F, w0t.rearrange("(k p) n -> p k n", p=P)),
                  (W1F, w1t.rearrange("(k p) n -> p k n", p=P)), (PW, pwp), (DW, dwp), (WOUT[:, :], woutt),
                  (WPD[:, :, :], wpd.rearrange("q p n -> p q n"))]
            ld += [(VEC[:, 0:7, :], vecs)]
            for d, s in ld:
                sp.dma_start(d, s).then_inc(s_load, 16)
            def raw(img):
                for h in range(2):
                    for k in range(KT):
                        cs = slice(h * NC // 2, (h + 1) * NC // 2)
                        sp.dma_start(RAW[:, cs, k, :],
                                     x_v[img, :, k, h * HALF:(h + 1) * HALF].rearrange("p (c n) -> p c n", n=C)
                                     ).then_inc(s_raw[h], 16)

            for q in range(PAIRS):
                sp.wait_ge(s_w1f, q + 1)
                sp.dma_start(w1_d[q], W1S[:, q, :, :, :].rearrange("p h k n -> p (h k n)")).then_inc(s_w1s, 16)
            sp.wait_ge(s_w1s, 16 * PAIRS)
            for n in range(PAIRS * CONVS):
                if n == CONVS:
                    raw(0)
                sp.wait_ge(s_low, n + 1)
                sp.dma_start(wc_d[n], CW[:, n % 2, :, :, :, :].rearrange("p g h x m -> p (g h x m)")).then_inc(s_wc[n % 2], 16)
            for m in range(2):
                sp.wait_ge(s_wc[m], 16 * PAIRS * CONVS // 2)

            def output_weights(pp, pair, q):
                sp.wait_ge(s_p, pp * QUADS + q + 1)
                sp.dma_start(WPA[:, q % 2, :], wpa[pair * QUADS + q]).then_inc(s_wpa[q % 2], 16)

            with sp.Fori(0, IMAGES) as img:
                for h in range(2):
                    sp.wait_ge(s_out[h], img * 16 + 16)
                    sp.dma_start(X[:, :, h * HALF:(h + 1) * HALF], x_v[img, :, :, h * HALF:(h + 1) * HALF]).then_inc(s_x[h], 16)
                with sp.Fori(0, PAIRS) as pair:
                    pp = img * PAIRS + pair
                    sp.wait_ge(s_pj, pp * TY * NC + 1)
                    sp.dma_start(W1[:, :, :, :, :].rearrange("p h k t n -> p (h k t n)"), w1_d[pair]).then_inc(s_w1, 16)
                    for n in range(CONVS):
                        q, ty = n // TY, n % TY
                        sp.wait_ge(s_conv, pp * CONVS + n + 1)
                        sp.dma_start(CW[:, n % 2, :, :, :, :].rearrange("p g h x m -> p (g h x m)"),
                                     wc_d[pair * CONVS + n]).then_inc(s_cw[n % 2], 16)
                        if q == 0:
                            sp.wait_ge(s_plo, pp * TY * NC + units_of(ty))
                        for g in range(4):
                            src = QKV[32 * q + 8 * g:32 * q + 8 * g + 8, ty, :, :, :, :]
                            for half in range(2):
                                sp.dma_start(CT[64 * half:64 * half + 64, n % 2, g, :],
                                             src[:, :, :, half:half + NB, :].rearrange("c h t b w -> c (h t) (b w)")
                                             ).then_inc(s_ct[n % 2], 16)
                        if ty == 0 and q >= 1:
                            output_weights(pp, pair, q - 1)
                    output_weights(pp, pair, QUADS - 1)
                sp.wait_ge(s_pj, (img + 1) * PAIRS * TY * NC + 1)
                for h in range(2):
                    for m in range(2):
                        sp.wait_ge(s_qa[h][m], (img + 1) * PAIRS * (QUADS // 2) * 16)
                raw((img + 1) % IMAGES)
                for h in range(2):
                    sp.wait_ge(s_fin, (img * PAIRS + 1) * 2 * NC + (h + 1) * NC + 3)
                    sp.dma_start(out_v[img, :, :, h * HALF:(h + 1) * HALF], X[:, :, h * HALF:(h + 1) * HALF]).then_inc(s_out[h], 16)
            for h in range(2):
                sp.wait_ge(s_out[h], 16 * IMAGES + 16)
                sp.wait_ge(s_raw[h], 16 * KT * (IMAGES + 1))

        @block.gpsimd
        def _(pool):
            pool.wait_ge(s_set, 1)
            pool.partition_all_reduce(MX[:, 1, :], MX[:, 0, :], P, RMAX).then_inc(s_allmax, 1)
            pool.memset(VTb[:, :, :, P:P + 1], 1.0).then_inc(s_one, 1)

            def take_q(pp, c):
                t, bh = c % RB, c // RB
                if c >= 3:
                    pool.wait_ge(s_fd, pp * NC + c - 2)
                    pool.wait_ge(s_fq, pp * NC + c - 2)
                elif c == 0:
                    pool.wait_ge(s_conv, pp * CONVS + CONVS + 2)
                pool.tensor_tensor(QF[:, c % 3, :].rearrange("p (b w) -> p b w", w=W),
                                   padded(2, 0, HB8 * bh, HB8, t), padded(2, 1, HB8 * bh, HB8, t),
                                   ALU.add).then_inc(s_qf, 1)

            def affine(c, s, signal, src):
                for k in range(KT):
                    pool.tensor_scalar(HB[:, s, k, :], src(k, c), RS[:, k:k + 1], NBI[:, k:k + 1],
                                       ALU.mult, ALU.add).then_inc(signal, 1)

            with pool.Fori(0, IMAGES) as img:
                gate(pool, s_gn, img * 2 + 1)
                for c in range(-2, NC):
                    if 0 <= c + 1 < NC:
                        if c + 1 >= NH:
                            gate(pool, s_lo, img * NC + c + 2 - NH)
                        affine(c + 1, (c + 1) % NH, s_h, lambda k, c: RAW[:, c, k, :])
                    if c + 2 < NC:
                        pool.wait_ge(s_sq, img * 2 * NC + 2 * (c + 2) + 2)
                        if c >= 0:
                            pool.wait_ge(s_ss, img * NC + c + 1)
                        pool.tensor_tensor(SQS[:, c % 2, :], SQ[:, c % 2, 0, :], SQ[:, c % 2, 1, :], ALU.add).then_inc(s_sqs, 1)
                for c in range(NC + 2):
                    d = c - 2
                    if d >= 0:
                        xs = X[:, :, d * C:(d + 1) * C]
                        pool.wait_ge(s_yn, img * NC + d + 1)
                        if d % (NC // 2) == 0:
                            pool.wait_ge(s_x[d // (NC // 2)], img * 16 + 16)
                        pool.tensor_tensor(xs, HB[:, d % NH, :, :], xs, ALU.add).then_inc(s_x1, 1)
                    if c < NC:
                        pool.wait_ge(s_ysq, img * 2 * NC + 2 * c + 2)
                        if c >= 2:
                            pool.wait_ge(s_yss, img * NC + c - 1)
                        pool.tensor_tensor(SQS[:, c % 2, :], SQ[:, c % 2, 0, :], SQ[:, c % 2, 1, :], ALU.add).then_inc(s_ysqs, 1)
                gate(pool, s_y, (img + 1) * NC)
                for ty in range(TY):
                    for t in range(RB):
                        row = QKV[:, ty, :, t, :, :]
                        pool.memset(row[:, :, :, 0:2], 0.0).then_inc(s_pad, 1)
                        pool.memset(row[:, :, :, WP - 2:WP], 0.0).then_inc(s_pad, 1)
                        edge = 0 if t < 2 else NB
                        pool.memset(row[:, :, edge, 2:2 + W], 0.0).then_inc(s_pad, 1)
                gate(pool, s_gn, img * 2 + 2)
                for c in range(NC):
                    if c >= NH:
                        gate(pool, s_lo1, img * NC + c + 1 - NH)
                    affine(c, c % NH, s_h1, lambda k, c: X[:, k, c * C:(c + 1) * C])
                gate(pool, s_h1, (img + 1) * KT * NC)
                for k in range(KT):
                    pool.tensor_scalar(X[:, k, :], X[:, k, :], VEC[:, 8, k:k + 1], None, ALU.add).then_inc(s_bias, 1)
                with pool.Fori(0, PAIRS) as pair:
                    pp = img * PAIRS + pair
                    for n in range(SLOTS):
                        for what, q, h in slot_steps(n):
                            if what == "den":
                                pool.wait_ge(s_dex, pp * 2 * QUADS + 2 * q + h + 1)
                                part = OQ[:, q % 2, h * C:(h + 1) * C]
                                pool.tensor_tensor(part, part, DN[:, h, :], ALU.mult).then_inc(s_qd, 1)
                            if what == "q":
                                take_q(pp, h)
                    for c in range(3, NC):
                        take_q(pp, c)

        def attend0(act, img, d):
            cols = slice(d * C, (d + 1) * C)
            act.wait_ge(s_kmx, img * NC + d + 1)
            act.activation(KBUF[:, cols], PS[:, 2 + d % 2, :], ACT.Copy).then_inc(s_kc, 1)
            act.wait_ge(s_vp, img * NC + d + 1)
            act.activation(VT[:, cols], PS[:, VBANK[d % 2], :], ACT.Copy, scale=KSC[:, 0:1]).then_inc(s_vc, 1)
            act.wait_ge(s_qsub, img * NC + d + 1)
            act.activation(QM[:, d % 2, :], QM[:, d % 2, :], ACT.Exp, scale=KSC[:, 0:1]).then_inc(s_qe, 1)

        @block.scalar
        def _(act):
            act.preload_act_table_set("natural_log_exp_and_others")
            for h in range(2):
                act.sem_inc(s_out[h], 16)
            act.wait_ge(s_load, 16 * 8)
            act.activation(I16[:, :], ident, ACT.Copy).then_inc(s_seta, 1)
            act.activation(VEC[:, 7, :], VEC[:, 6, :], ACT.Ln, bias=const(E_GN)).then_inc(s_seta, 1)
            act.wait_ge(s_seta, 2)
            act.activation(VEC[:, 7, :], VEC[:, 7, :], ACT.Exp, scale=-0.5).then_inc(s_seta, 1)
            for n in range(PAIRS * CONVS):
                act.wait_ge(s_tw, 4 * (n + 1))
                if n >= 2:
                    act.wait_ge(s_wc[n % 2], 16 * (n // 2))
                act.activation(CW[:, n % 2, :, 0, :, :].rearrange("p g x m -> p g (x m)"), TF[:, n % 2, :, :], ACT.Copy).then_inc(s_hiw, 1)

            def rstd(count):
                act.wait_ge(s_gvar, count)
                act.activation(RS[:, :], G4[:, 2, :], ACT.Ln, bias=const(E_GN)).then_inc(s_gln, 1)
                act.wait_ge(s_gln, count)
                act.activation(RS[:, :], RS[:, :], ACT.Exp, scale=-0.5).then_inc(s_grs, 1)

            def rms(c, img, ready, ln, inv, used, shift):
                act.wait_ge(ready, img * NC + c + 1)
                if c >= 2:
                    act.wait_ge(used, img * NC + c - 1)
                act.activation(INV[:, c % 2, :], PS[:, c % 2, :], ACT.Ln, bias=const(E_RMS)).then_inc(ln, 1)
                act.wait_ge(ln, img * NC + c + 1)
                act.activation(INV[:, c % 2, :], INV[:, c % 2, :], ACT.Exp, scale=-0.5, bias=const(shift)).then_inc(inv, 1)

            def invert(pp, c):
                act.wait_ge(s_fd, pp * NC + c + 1)
                if c >= 2:
                    act.wait_ge(s_fq, pp * NC + c - 1)
                act.activation(FD[:, c % 2, :], PS[:, 4 + c % 2, :], ACT.Ln, bias=const(E_DEN)).then_inc(s_fln, 1)
                act.wait_ge(s_fln, pp * NC + c + 1)
                act.activation(FD[:, c % 2, :], FD[:, c % 2, :], ACT.Exp, scale=-1.0).then_inc(s_fex, 1)

            rstd(1)
            with act.Fori(0, IMAGES) as img:
                act.wait_ge(s_gn, img * 2 + 1)
                for c in range(-2, NC + 5):
                    if c == 1:
                        act.wait_ge(s_xn, img * NC + c)
                        act.activation(XN[:, c - 1, 0, :, :], HB[:, (c - 1) % NH, :, :], ACT.Copy).then_inc(s_hi, 1)
                    if 0 <= c < NC:
                        rms(c, img, s_ss, s_ln, s_inv, s_xn, L_XS0)
                    if 1 < c <= NC:
                        act.wait_ge(s_xn, img * NC + c)
                        act.activation(XN[:, c - 1, 0, :, :], HB[:, (c - 1) % NH, :, :], ACT.Copy).then_inc(s_hi, 1)
                    if 0 <= c - 3 < NC:
                        attend0(act, img, c - 3)
                    if c == NC + 4:
                        for h in range(EK):
                            act.wait_ge(s_kb, img + 1)
                            kh = KBUF[:, h * N // EK:(h + 1) * N // EK]
                            act.activation(kh, kh, ACT.Exp, scale=KSC[:, 0:1], bias=KB[:, 1:2], accum_out=SK[:, h:h + 1]).then_inc(s_ke, 1)
                    if 0 <= c - 5 < NC:
                        act.wait_ge(s_qt, img * NC + c - 4)
                        act.activation(QS[:, (c - 5) * C:(c - 4) * C], PS[:, 6, :], ACT.Copy).then_inc(s_qs, 1)
                    if c + 2 < NC:
                        if c + 2 >= 2:
                            act.wait_ge(s_sqs, img * NC + c + 1)
                        for k in range(KT):
                            act.activation(SQ[:, c % 2, k, :], RAW[:, c + 2, k, :], ACT.Square, scale=RS[:, k:k + 1],
                                           bias=NBI[:, k:k + 1]).then_inc(s_sq, 1)
                for c in range(NC + 2):
                    if c < NC:
                        act.wait_ge(s_y, img * NC + c + 1)
                        if c >= NH:
                            act.wait_ge(s_x1, img * NC + c + 1 - NH)
                        for k in range(KT):
                            act.activation(HB[:, c % NH, k, :], PS[:, 2 + 2 * (c % 2) + k, :], ACT.Identity,
                                           scale=VEC[:, 2, k:k + 1], bias=VEC[:, 9, k:k + 1]).then_inc(s_yb, 1)
                        if c >= 2:
                            act.wait_ge(s_ysqs, img * NC + c - 1)
                        for k in range(KT):
                            act.activation(SQ[:, c % 2, k, :], PS[:, 2 + 2 * (c % 2) + k, :], ACT.Square,
                                           bias=VEC[:, 1, k:k + 1]).then_inc(s_ysq, 1)
                    if 0 <= c - 1 < NC:
                        rms(c - 1, img, s_yss, s_yln, s_yinv, s_yn, L_RMS)
                rstd(img * 2 + 2)
                for c in range(NC):
                    act.wait_ge(s_h1, img * 2 * NC + 2 * c + 2)
                    act.activation(XN[:, c, 0, :, :], HB[:, c % NH, :, :], ACT.Copy).then_inc(s_hi1, 1)
                act.wait_ge(s_pad, (img + 1) * TY * RB * 3)
                with act.Fori(0, PAIRS) as pair:
                    pp = img * PAIRS + pair
                    for n in range(TY * NC):
                        ty, t, bh = unit(n)
                        act.wait_ge(s_pj, pp * TY * NC + n + 2)
                        act.activation(padded(ty, 0, HB8 * bh, HB8, t), PS[:, n % 4, :].rearrange("p (b w) -> p b w", w=W),
                                       ACT.Copy, scale=PROJ).then_inc(s_phi, 1)
                    for u in range(DU):
                        act.wait_ge(s_dt, pp * DU + u + 1)
                        if u >= 2:
                            act.wait_ge(s_dkv, pp * DU + u - 1)
                        act.activation(KTb[0:TP, u % 2, :, :].rearrange("p j m -> p (j m)"), PS[0:TP, DBANK[u % 2], :], ACT.Relu,
                                       scale=MX[0:TP, 1, 1:2]).then_inc(s_dk, 1)
                    for n in range(SLOTS):
                        for what, q, h in slot_steps(n):
                            i = pp * 2 * QUADS + 2 * q + h
                            if what == "trans":
                                act.wait_ge(s_at, i + 1)
                                if 2 * q + h >= 2:
                                    act.wait_ge(s_akv, i - 1)
                                act.activation(KTb[:, h, :, :].rearrange("p j m -> p (j m)"), PS[:, 4, :], ACT.Copy).then_inc(s_ak, 1)
                            if what == "den":
                                act.wait_ge(s_den, i + 1)
                                if q >= 1:
                                    act.wait_ge(s_qd, i - 1)
                                act.activation(DN[:, h, :], PS[:, 7, :], ACT.Ln, bias=const(E_DEN)).then_inc(s_dln, 1)
                                act.wait_ge(s_dln, i + 1)
                                act.activation(DN[:, h, :], DN[:, h, :], ACT.Exp, scale=-1.0).then_inc(s_dex, 1)
                            if what == "fd":
                                invert(pp, h)
                        for what, q, h in slot_steps(n):
                            if what == "den":
                                act.wait_ge(s_qd, pp * 2 * QUADS + 2 * q + h + 1)
                                act.dma_start(QA[32 * q:32 * q + 32, :, h * C:(h + 1) * C],
                                              OQ[:, q % 2, h * C:(h + 1) * C]).then_inc(s_qa[h][q % 2], 16)
                        if n < CONVS and n % TY != 1:
                            q, ty = n // TY, n % TY
                            act.wait_ge(s_conv, pp * CONVS + n + 3)
                            if ty == 0 and q >= 1:
                                act.wait_ge(s_at, pp * 2 * QUADS + 2 * q)
                            if ty == 2 and q >= 2:
                                for h in range(2):
                                    act.wait_ge(s_qa[h][q % 2], (pp * (QUADS // 2) + q // 2) * 16)
                            act.activation((OK[:, :] if ty == 0 else OQ[:, q % 2, :]).rearrange("p (a b) -> p a b", a=2),
                                           PS[:, 2 * (n % 2):2 * (n % 2) + 2, :], ACT.Relu, scale=SCA[:, 0:1]).then_inc(s_ev[ty], 1)
                    for c in range(2, NC):
                        invert(pp, c)
                rstd(img * 2 + 3)

        @block.vector
        def _(dve):
            V = nc.vector
            chain = [0]

            def link(ins):
                chain[0] += 1
                ins.then_inc(s_setg, 1)
                dve.wait_ge(s_setg, chain[0])

            dve.sem_inc(s_pj, 1)
            dve.sem_inc(s_conv, 2)
            dve.sem_inc(s_p, 2)
            dve.sem_inc(s_fin, 3)
            dve.wait_ge(s_load, 16 * 8)
            for k in range(KT):
                link(V.tensor_scalar(W0F[:, k, :], W0F[:, k, :], VEC[:, 0, k:k + 1], CH ** 0.5, ALU.mult, ALU.mult))
            for j, a in enumerate((W0F, W1F, PW, DW)):
                link(V.tensor_reduce(MX[:, 0, j:j + 1], a if j > 1 else a.rearrange("p k n -> p (k n)"), AX, ALU.max,
                                     apply_absolute_value=True))
            V.tensor_scalar(SK[:, 0:1], MX[:, 0, 0:1], 1.0, None, ALU.mult).then_inc(s_set, 1)
            dve.wait_ge(s_allmax, 1)
            link(V.tensor_scalar(MX[:, 1, :], MX[:, 1, :], 1e-30, None, ALU.max))
            link(V.reciprocal(MX[:, 2, :], MX[:, 1, :]))
            link(V.tensor_scalar(KSC[:, :], MX[:, 1, 0:1], 1.0 / (WS * XS0), None, ALU.mult))
            link(V.tensor_tensor(SCA[:, :], MX[:, 1, 1:2], MX[:, 1, 2:3], ALU.mult))
            link(V.tensor_scalar(SCA[:, :], SCA[:, :], MX[:, 1, 3:4], 1.0 / WS, ALU.mult, ALU.mult))
            link(V.tensor_scalar(PW, PW, MX[:, 2, 2:3], WS, ALU.mult, ALU.mult))
            link(V.tensor_scalar(DW, DW, MX[:, 2, 3:4], None, ALU.mult))
            link(V.tensor_scalar(W0F, W0F, MX[:, 2, 0:1], WS, ALU.mult, ALU.mult))
            link(V.tensor_copy(W0[:, 0, :, :], W0F))
            link(V.tensor_tensor(W0[:, 1, :, :], W0F, W0[:, 0, :, :], ALU.subtract))
            link(V.tensor_scalar(W1F, W1F, MX[:, 2, 1:2], WS, ALU.mult, ALU.mult))
            for q in range(PAIRS):
                part = W1F[:, :, q * TY * P:(q + 1) * TY * P]
                link(V.tensor_copy(W1S[:, q, 0, :, :], part))
                V.tensor_tensor(W1S[:, q, 1, :, :], part, W1S[:, q, 0, :, :], ALU.subtract).then_inc(s_w1f, 1)
            dve.wait_ge(s_seta, 3)
            link(V.tensor_tensor(VEC[:, 7, :], VEC[:, 7, :], VEC[:, 3, :], ALU.mult))
            link(V.tensor_tensor(VEC[:, 9, :], VEC[:, 1, :], VEC[:, 2, :], ALU.mult))
            link(V.tensor_tensor(VEC[:, 8, :], VEC[:, 5, :], VEC[:, 7, :], ALU.mult))
            link(V.tensor_tensor(VEC[:, 8, :], VEC[:, 4, :], VEC[:, 8, :], ALU.subtract))
            pwv = PW.rearrange("p (g x o t) -> p g x o t", o=8, x=1, t=1)
            dwv = DW.rearrange("p (g x o t) -> p g x o t", x=TAPS, o=1, t=RB)
            for n in range(PAIRS * CONVS + 1):
                if n < PAIRS * CONVS:
                    for g in range(4):
                        if n >= 2:
                            dve.wait_ge(s_low, n - 1)
                        V.tensor_tensor(TF[:, n % 2, g, :].rearrange("p (x o t) -> p x o t", x=TAPS, t=RB),
                                        bc(pwv[:, 4 * n + g], [P, TAPS, 8, RB]), bc(dwv[:, 4 * n + g], [P, TAPS, 8, RB]),
                                        ALU.mult).then_inc(s_tw, 1)
                m = n - 1
                if m >= 0:
                    dve.wait_ge(s_hiw, m + 1)
                    V.tensor_tensor(CW[:, m % 2, :, 1, :, :].rearrange("p g x m -> p g (x m)"), TF[:, m % 2, :, :],
                                    CW[:, m % 2, :, 0, :, :].rearrange("p g x m -> p g (x m)"), ALU.subtract).then_inc(s_low, 1)

            def stats(c, src):
                for k in range(KT):
                    V.bn_stats(ST[:, k, c, :], src(k, c)).then_inc(s_bn, 1)

            def of_raw(k, c):
                return RAW[:, c, k, :]

            def of_x(k, c):
                return X[:, k, c * C:(c + 1) * C]

            LINKS = 7

            def step(ins, value):
                ins.then_inc(s_dchain, 1)
                dve.wait_ge(s_dchain, value)

            def moments(count):
                done = (count - 1) * LINKS
                gate(dve, s_bn, count * KT * NC)
                V.bn_aggr(MV[:, 0, :], ST[:, 0, :, :].rearrange("p a b -> p (a b)")).then_inc(s_dchain, 1)
                step(V.bn_aggr(MV[:, 1, :], ST[:, 1, :, :].rearrange("p a b -> p (a b)")), done + 2)
                step(V.tensor_copy(G4[:, 0, :], MV[:, :, 0]), done + 3)
                step(V.tensor_tensor(G4[:, 1, :], MV[:, :, 0], MV[:, :, 0], ALU.mult), done + 4)
                V.tensor_tensor(G4[:, 1, :], MV[:, :, 1], G4[:, 1, :], ALU.add).then_inc(s_gin, 1)

            def variance(count):
                done = (count - 1) * LINKS + 4
                dve.wait_ge(s_gavg, count)
                step(V.tensor_copy(G4[:, 0:2, :], PS[:, 7, 0:4].rearrange("p (a b) -> p a b", a=2)), done + 1)
                step(V.tensor_tensor(G4[:, 2, :], G4[:, 0, :], G4[:, 0, :], ALU.mult), done + 2)
                V.tensor_tensor(G4[:, 2, :], G4[:, 1, :], G4[:, 2, :], ALU.subtract).then_inc(s_gvar, 1)

            def affine_map(count, scale):
                dve.wait_ge(s_grs, count)
                step(V.tensor_scalar(RS[:, :], RS[:, :], scale, None, ALU.mult), count * LINKS)
                V.scalar_tensor_tensor(out=NBI[:, :], in0=G4[:, 0, :], scalar=-1.0, in1=RS[:, :], op0=ALU.mult,
                                       op1=ALU.mult).then_inc(s_gn, 1)

            for h in range(2):
                dve.wait_ge(s_raw[h], 16 * KT)
                for c in range(h * NC // 2, (h + 1) * NC // 2):
                    stats(c, of_raw)
            moments(1)
            variance(1)
            affine_map(1, 1.0)
            def relu_q(pp, c):
                dve.wait_ge(s_qf, pp * NC + c + 1)
                V.tensor_scalar(QF[:, c % 3, :], QF[:, c % 3, :], 0.0, MX[:, 1, 1:2], ALU.max, ALU.mult).then_inc(s_qrl, 1)

            def attend1(pp):
                for n in range(TY * NC):
                    ty, t, bh = unit(n)
                    dve.wait_ge(s_phi, pp * TY * NC + n + 1)
                    V.scalar_tensor_tensor(out=padded(ty, 1, HB8 * bh, HB8, t),
                                           in0=PS[:, n % 4, :].rearrange("p (b w) -> p b w", w=W), scalar=PROJ,
                                           in1=padded(ty, 0, HB8 * bh, HB8, t), op0=ALU.mult,
                                           op1=ALU.subtract).then_inc(s_plo, 1)
                for u in range(DU):
                    dve.wait_ge(s_dt, pp * DU + u + 1)
                    if u >= 2:
                        dve.wait_ge(s_dkv, pp * DU + u - 1)
                    V.tensor_scalar(VTb[0:TP, u % 2, :, 0:P], PS[0:TP, DBANK[u % 2] + 1, :].rearrange("p (j m) -> p j m", j=4),
                                    MX[0:TP, 1, 1:2], None, ALU.mult).then_inc(s_dv, 1)
                dve.wait_ge(s_dkv, pp * DU + DU)
                V.tensor_tensor(KVM[:, :], PS[:, 7, 0:P], m8, ALU.mult).then_inc(s_dkm, 1)
                V.tensor_copy(KS[:, 0:1], PS[:, 7, P:P + 1]).then_inc(s_dks, 1)
                dve.wait_ge(s_dks, pp * 2 + 1)
                V.tensor_scalar(DMD[:, :], m8, KS[:, 0:1], None, ALU.mult).then_inc(s_dks, 1)
                for n in range(SLOTS):
                    for what, q, h in slot_steps(n):
                        i = pp * 2 * QUADS + 2 * q + h
                        if what == "trans":
                            dve.wait_ge(s_at, i + 1)
                            if 2 * q + h >= 2:
                                dve.wait_ge(s_akv, i - 1)
                            V.tensor_copy(VTb[:, h, :, 0:P], PS[:, 5, :].rearrange("p (j m) -> p j m", j=4)).then_inc(s_av, 1)
                        if what == "kv" and h == 1:
                            dve.wait_ge(s_akv, i + 1)
                            V.tensor_tensor(KVM[:, :], PS[:, 6, 0:P], mgt, ALU.mult).then_inc(s_kvm, 1)
                            V.tensor_copy(KS[:, 0:1], PS[:, 6, P:P + 1]).then_inc(s_kvm, 1)
                        if what == "sel":
                            j = pp * QUADS + q
                            dve.wait_ge(s_sel, j + 1)
                            V.tensor_copy(KVS[:, 0:32], PS[:, 6, CH:CH + 32]).then_inc(s_kvs, 1)
                            V.tensor_copy(KS[:, 1:2], PS[:, 6, CH + 32:CH + 33]).then_inc(s_kvs, 1)
                            dve.wait_ge(s_kvs, j * 3 + 2)
                            if q >= 1:
                                dve.wait_ge(s_den, pp * 2 * QUADS + 2 * q)
                            V.tensor_scalar(DM[:, :], mgt, KS[:, 1:2], None, ALU.mult).then_inc(s_kvs, 1)
                        if what == "p":
                            dve.wait_ge(s_p, pp * QUADS + q + 3)
                            V.tensor_copy(PA[32 * q:32 * q + 32, :], PS[32 * q:32 * q + 32, 6, CH:2 * CH]).then_inc(s_pa, 1)
                        if what == "turn":
                            dve.wait_ge(s_dtr, pp + 1)
                            V.tensor_copy(KVS[:, :], PS[:, 6, 0:P]).then_inc(s_dkm, 1)
                        if what == "weights":
                            dve.wait_ge(s_dp, pp + 1)
                            V.tensor_copy(PD[:, :], PS[:, 6, CH:2 * CH]).then_inc(s_pd, 1)
                        if what == "q":
                            relu_q(pp, h)
                    if n < CONVS and n % TY == 1:
                        q = n // TY
                        dve.wait_ge(s_conv, pp * CONVS + n + 3)
                        if q >= 1:
                            dve.wait_ge(s_at, pp * 2 * QUADS + 2 * q)
                        V.tensor_scalar(OV[:, :].rearrange("p (a b) -> p a b", a=2), PS[:, 2 * (n % 2):2 * (n % 2) + 2, :],
                                        SCA[:, 0:1], None, ALU.mult).then_inc(s_ev[1], 1)

            STATS = {3: (0,), 4: (1, 2), 5: (3,), 6: (4, 5), 7: (6, 7)}

            def finish(img, pp, last):
                for c in range(1, NC + 2):
                    d = c - 1
                    if 0 <= d < NC:
                        dve.wait_ge(s_fex, pp * NC + d + 1)
                        if d >= 2:
                            dve.wait_ge(s_fo, pp * NC + d - 1)
                        V.tensor_tensor(QN[:, d % 2, :], QF[:, d % 3, :], FD[:, d % 2, :], ALU.mult).then_inc(s_fq, 1)
                    if c + 2 < NC:
                        relu_q(pp, c + 2)
                    d = c - 2
                    if d >= 0:
                        t, bh = d % RB, d // RB
                        dve.wait_ge(s_fo, pp * NC + d + 1)
                        dve.wait_ge(s_bias, (img + 1) * KT)
                        for k in range(KT):
                            xs = rows(X[:, k, :], HB8 * bh, HB8, t)
                            V.scalar_tensor_tensor(out=xs, in0=PS[:, 2 * (d % 2) + k, :].rearrange("p (b w) -> p b w", w=W),
                                                   scalar=VEC[:, 7, k:k + 1], in1=xs, op0=ALU.mult, op1=ALU.add).then_inc(s_fin, 1)
                    if last and c in STATS:
                        for e in STATS[c]:
                            if e % (NC // 2) == 0:
                                dve.wait_ge(s_raw[e // (NC // 2)], (img + 2) * 16 * KT)
                            stats(e, of_raw)
                    if last and c == NC - 1:
                        moments(img * 2 + 3)
                    if last and c == NC:
                        variance(img * 2 + 3)
                if last:
                    affine_map(img * 2 + 3, 1.0)

            with dve.Fori(0, IMAGES) as img:
                for c in range(NC + 5):
                    d = c - 3
                    if 0 <= d < NC:
                        dve.wait_ge(s_kp, img * NC + d + 1)
                        V.tensor_reduce(KMX[:, d:d + 1], PS[:, 2 + d % 2, :], AX, ALU.max).then_inc(s_kmx, 1)
                        qv = PS[:, 4, :].rearrange("p (j h d) -> p j h d", j=4, d=D0)
                        dve.wait_ge(s_qp, img * NC + d + 1)
                        V.tensor_reduce(QX[:, d % 2, :, :], qv, AX, ALU.max).then_inc(s_qmx, 1)
                        dve.wait_ge(s_qmx, img * NC + d + 1)
                        if d >= 2:
                            dve.wait_ge(s_qt, img * NC + d - 1)
                        V.tensor_tensor(QM[:, d % 2, :].rearrange("p (j h d) -> p j h d", j=4, d=D0), qv,
                                        bc(QX[:, d % 2, :, :].rearrange("p j (h o) -> p j h o", o=1), [P, 4, HEADS0, D0]),
                                        ALU.subtract).then_inc(s_qsub, 1)
                    if c == NC + 3:
                        dve.wait_ge(s_kmx, img * NC + NC)
                        V.tensor_reduce(KB[:, 0:1], KMX[:, :], AX, ALU.max).then_inc(s_sk, 1)
                        dve.wait_ge(s_sk, img * 3 + 1)
                        dve.wait_ge(s_kc, img * NC + NC)
                        V.scalar_tensor_tensor(out=KB[:, 1:2], in0=KB[:, 0:1], scalar=-1.0, in1=KSC[:, 0:1], op0=ALU.mult,
                                               op1=ALU.mult).then_inc(s_kb, 1)
                    d = c - 4
                    if 0 <= d < NC:
                        qm = QM[:, d % 2, :].rearrange("p (j h d) -> p j h d", j=4, d=D0)
                        dve.wait_ge(s_qe, img * NC + d + 1)
                        V.tensor_reduce(QSM[:, d % 2, :, :], qm, AX, ALU.add).then_inc(s_qsum, 1)
                        dve.wait_ge(s_qsum, img * NC + d + 1)
                        V.reciprocal(QR[:, d % 2, :, :], QSM[:, d % 2, :, :]).then_inc(s_qr, 1)
                        dve.wait_ge(s_qr, img * NC + d + 1)
                        V.tensor_tensor(qm, qm, bc(QR[:, d % 2, :, :].rearrange("p j (h o) -> p j h o", o=1), [P, 4, HEADS0, D0]),
                                        ALU.mult).then_inc(s_qn, 1)
                    if c < NC:
                        hb = HB[:, c % NH, :, :]
                        dve.wait_ge(s_h, img * 2 * NC + 2 * c + 2)
                        dve.wait_ge(s_inv, img * NC + c + 1)
                        V.tensor_tensor(hb, hb, bc(INV[:, c % 2:c % 2 + 1, :], [P, KT, C]), ALU.mult).then_inc(s_xn, 1)
                    if 1 <= c <= NC:
                        dve.wait_ge(s_hi, img * NC + c)
                        V.tensor_tensor(XN[:, c - 1, 1, :, :], HB[:, (c - 1) % NH, :, :], XN[:, c - 1, 0, :, :], ALU.subtract).then_inc(s_lo, 1)
                for d in range(NC):
                    dve.wait_ge(s_ket, img * NC + d + 1)
                    if d >= 2:
                        dve.wait_ge(s_ctx, img * NC + d - 1)
                    V.tensor_copy(EKT[:, d % 2, :, :].rearrange("p j m -> p (j m)"), PS[:, 2 + d % 2, :]).then_inc(s_ekt, 1)
                dve.wait_ge(s_ke, img * EK + EK)
                V.tensor_reduce(SK[:, EK:EK + 1], SK[:, 0:EK], AX, ALU.add).then_inc(s_sk, 1)
                dve.wait_ge(s_sk, img * 3 + 2)
                V.reciprocal(SK[:, EK + 1:EK + 2], SK[:, EK:EK + 1]).then_inc(s_sk, 1)
                dve.wait_ge(s_ctx, img * NC + NC)
                V.tensor_tensor(SM, PS[:, 7, 0:P], m32, ALU.mult).then_inc(s_sm, 1)
                dve.wait_ge(s_mp, img + 1)
                dve.wait_ge(s_sk, img * 3 + 3)
                V.tensor_scalar(MM, PS[:, 6, 0:CH], SK[:, EK + 1:EK + 2], D0 ** -0.5, ALU.mult, ALU.mult).then_inc(s_mm, 1)
                for c in range(NC + 2):
                    if c < NC:
                        hb = HB[:, c % NH, :, :]
                        dve.wait_ge(s_yb, img * 2 * NC + 2 * c + 2)
                        dve.wait_ge(s_yinv, img * NC + c + 1)
                        V.tensor_tensor(hb, hb, bc(INV[:, c % 2:c % 2 + 1, :], [P, KT, C]), ALU.mult).then_inc(s_yn, 1)
                    if c >= 2:
                        dve.wait_ge(s_x1, img * NC + c - 1)
                        stats(c - 2, of_x)
                moments(img * 2 + 2)
                variance(img * 2 + 2)
                affine_map(img * 2 + 2, XS1)
                for c in range(NC):
                    dve.wait_ge(s_hi1, img * NC + c + 1)
                    V.tensor_tensor(XN[:, c, 1, :, :], HB[:, c % NH, :, :], XN[:, c, 0, :, :], ALU.subtract).then_inc(s_lo1, 1)
                with dve.Fori(0, PAIRS - 1) as pair:
                    attend1(img * PAIRS + pair)
                    finish(img, img * PAIRS + pair, False)
                attend1(img * PAIRS + PAIRS - 1)
                finish(img, img * PAIRS + PAIRS - 1, True)

        @block.tensor
        def _(pe):
            MM_ = nc.tensor.matmul
            SPLIT = ((0, 0), (1, 0), (0, 1))

            def gavg(count):
                pe.wait_ge(s_gin, count)
                MM_(PS[:, 7, 0:4], g8, G4[:, 0:2, :].rearrange("p a b -> p (a b)"), start=True, stop=True).then_inc(s_gavg, 1)

            def total(img, c, ready, signal, used):
                pe.wait_ge(ready, img * NC + c + 1)
                if c >= 2:
                    pe.wait_ge(used, img * NC + c - 1)
                MM_(PS[:, c % 2, :], ones, SQS[:, c % 2, :], start=True, stop=True).then_inc(signal, 1)

            def turn_q(img, d):
                pe.wait_ge(s_qn, img * NC + d + 1)
                if d >= 1:
                    pe.wait_ge(s_qs, img * NC + d)
                for j in range(4):
                    last = nc.tensor.transpose(PS[:, 6, j * P:(j + 1) * P], QM[:, d % 2, j * P:(j + 1) * P], ident)
                last.then_inc(s_qt, 1)

            def project0(img, d):
                pe.wait_ge(s_lo, img * NC + d + 1)
                if d >= 2:
                    pe.wait_ge(s_kmx, img * NC + d - 1)
                    pe.wait_ge(s_kc, img * NC + d - 1)
                i = 0
                for k in range(KT):
                    for a, b in SPLIT:
                        last = MM_(PS[:, 2 + d % 2, :], W0[:, a, k, HID:2 * HID], XN[:, d, b, k, :],
                                   start=(i == 0), stop=(i == 3 * KT - 1))
                        i += 1
                last.then_inc(s_kp, 1)
                for bank, o, free, signal, ring in ((VBANK[d % 2], 2 * HID, s_vc, s_vp, 2), (4, 0, s_qsub, s_qp, 1)):
                    if d >= ring:
                        pe.wait_ge(free, img * NC + d + 1 - ring)
                    for j in range(4):
                        i = 0
                        for k in range(KT):
                            for a, b in SPLIT:
                                last = MM_(PS[:, bank, j * P:(j + 1) * P], XN[:, d, b, k, j * P:(j + 1) * P], W0[:, a, k, o:o + HID],
                                           start=(i == 0), stop=(i == 3 * KT - 1))
                                i += 1
                    last.then_inc(signal, 1)

            def denominator(pp, c):
                pe.wait_ge(s_qrl, pp * NC + c + 1)
                if c >= 2:
                    pe.wait_ge(s_fln, pp * NC + c - 1)
                else:
                    pe.wait_ge(s_ak, (pp + 1) * 2 * QUADS)
                    pe.wait_ge(s_av, (pp + 1) * 2 * QUADS)
                MM_(PS[:, 4 + c % 2, :], DMD[:, :], QF[:, c % 3, :], start=True, stop=True).then_inc(s_fd, 1)

            def attend1(img, pair):
                pp = img * PAIRS + pair
                pe.wait_ge(s_w1, pp * 16 + 16)
                for n in range(TY * NC):
                    ty, t, bh = unit(n)
                    if n in (0, 2):
                        pe.wait_ge(s_fin, pp * 2 * NC + 1 + n)
                    if n % (RB * TY) == 0:
                        pe.wait_ge(s_lo1, img * NC + (bh + 1) * NC // 2)
                    if n >= 4:
                        pe.wait_ge(s_plo, pp * TY * NC + n - 3)
                    i = 0
                    for k in range(KT):
                        for a, b in SPLIT:
                            last = MM_(PS[:, n % 4, :].rearrange("p (c b w) -> p c b w", c=NC // 2, w=W), W1[:, a, k, ty, :],
                                       half_rows(b, k, bh, t), start=(i == 0), stop=(i == 3 * KT - 1))
                            i += 1
                    last.then_inc(s_pj, 1)
                for u in range(DU + 1):
                    if u < DU:
                        if u == 0:
                            pe.wait_ge(s_plo, pp * TY * NC + units_of(1))
                        elif u == 1:
                            pe.wait_ge(s_plo, pp * TY * NC + TY * NC - 2)
                        else:
                            pe.wait_ge(s_dk, pp * DU + u - 1)
                            pe.wait_ge(s_dv, pp * DU + u - 1)
                        for ty in range(2):
                            for j in range(4):
                                for a in range(2):
                                    last = MM_(PS[0:TP, DBANK[u % 2] + ty, j * P:(j + 1) * P], stretch(ty, a, 4 * u + j), I16[:, :],
                                               start=(a == 0), stop=(a == 1))
                        last.then_inc(s_dt, 1)
                    v = u - 1
                    if v >= 0:
                        pe.wait_ge(s_dk, pp * DU + v + 1)
                        pe.wait_ge(s_dv, pp * DU + v + 1)
                        for j in range(4):
                            last = MM_(PS[:, 7, 0:P + 1], KTb[0:TP, v % 2, j, :], VTb[0:TP, v % 2, j, :],
                                       start=(v == 0 and j == 0), stop=(v == DU - 1 and j == 3))
                        last.then_inc(s_dkv, 1)
                for n in range(SLOTS):
                    for what, q, h in slot_steps(n):
                        i = pp * 2 * QUADS + 2 * q + h
                        j4 = pp * QUADS + q
                        if what == "trans":
                            pe.wait_ge(s_ev[0], j4 + 1)
                            pe.wait_ge(s_ev[1], j4 + 1)
                            if 2 * q + h >= 1:
                                pe.wait_ge(s_ak, i)
                                pe.wait_ge(s_av, i)
                            for src, bank in ((OK, 4), (OV, 5)):
                                for j in range(4):
                                    at = h * C + j * P
                                    last = nc.tensor.transpose(PS[:, bank, j * P:(j + 1) * P], src[:, at:at + P], ident)
                            last.then_inc(s_at, 1)
                        if what == "kv":
                            pe.wait_ge(s_ak, i + 1)
                            pe.wait_ge(s_av, i + 1)
                            if h == 0:
                                if q >= 1:
                                    pe.wait_ge(s_pa, j4)
                                else:
                                    pe.wait_ge(s_pd, pp + 1)
                            for j in range(4):
                                last = MM_(PS[:, 6, 0:P + 1], KTb[:, h, j, :], VTb[:, h, j, :],
                                           start=(h == 0 and j == 0), stop=(h == 1 and j == 3))
                            last.then_inc(s_akv, 1)
                        if what == "sel":
                            pe.wait_ge(s_kvm, j4 * 2 + 2)
                            MM_(PS[:, 6, CH:CH + 32], KVM[:, :], sel, start=True, stop=True)
                            MM_(PS[:, 6, CH + 32:CH + 33], tsum, KS[:, 0:1], start=True, stop=True).then_inc(s_sel, 1)
                        if what == "p":
                            pe.wait_ge(s_wpa[q % 2], (pp * (QUADS // 2) + q // 2 + 1) * 16)
                            MM_(PS[32 * q:32 * q + 32, 6, CH:2 * CH], KVS[:, 0:32], WPA[:, q % 2, :], start=True,
                                stop=True).then_inc(s_p, 1)
                        if what == "turn":
                            pe.wait_ge(s_dkm, pp * 2 + 1)
                            MM_(PS[:, 6, 0:P], KVM[:, :], ident, start=True, stop=True).then_inc(s_dtr, 1)
                        if what == "weights":
                            pe.wait_ge(s_dkm, pp * 2 + 2)
                            nc.tensor.matmul(PS[:, 6, CH:2 * CH], KVS[:, :], WPD[:, pair, :], start=True, stop=True).then_inc(s_dp, 1)
                        if what == "fd":
                            denominator(pp, h)
                        if what == "den":
                            pe.wait_ge(s_ev[2], j4 + 1)
                            if h == 0:
                                pe.wait_ge(s_kvs, j4 * 3 + 3)
                            if 2 * q + h >= 1:
                                pe.wait_ge(s_dln, i)
                            MM_(PS[:, 7, :], DM[:, :], OQ[:, q % 2, h * C:(h + 1) * C], start=True, stop=True).then_inc(s_den, 1)
                    if n < CONVS:
                        m = n % 2
                        q, ty = n // TY, n % TY
                        uses = CONVS // 2
                        pe.wait_ge(s_cw[m], (pp * uses + n // 2 + 1) * 16)
                        pe.wait_ge(s_ct[m], (pp * uses + n // 2 + 1) * 128)
                        if n >= 2:
                            pq, pt = (n - 2) // TY, (n - 2) % TY
                            pe.wait_ge(s_ev[pt], pp * QUADS + pq + 1)
                        for ch in range(2):
                            i = 0
                            for a in range(2):
                                for dx in range(TAPS):
                                    for g in range(4):
                                        mv = CT[:, m, g, :].rearrange("p (b w) -> p b w", w=WP)[:, ch * HB8:(ch + 1) * HB8, dx:dx + W]
                                        last = MM_(PS[32 * g:32 * g + 32, 2 * m + ch, :].rearrange("p (b w) -> p b w", w=W),
                                                   CW[:, m, g, a, dx, :], mv, start=(i == 0), stop=(i == 2 * TAPS - 1))
                                    i += 1
                        last.then_inc(s_conv, 1)

            def finish(img, pp, last_pair):
                for c in range(1, NC + 1):
                    if c + 1 < NC:
                        denominator(pp, c + 1)
                    if last_pair and c == NC:
                        gavg(img * 2 + 3)
                    d = c - 1
                    if d >= 0:
                        t, bh = d % RB, d // RB
                        pe.wait_ge(s_fq, pp * NC + d + 1)
                        if d >= 2:
                            pe.wait_ge(s_fin, pp * 2 * NC + 2 * (d - 1) + 3)
                        for k in range(KT):
                            MM_(PS[:, 2 * (d % 2) + k, :], PD[:, k * P:(k + 1) * P], QN[:, d % 2, :], start=True, stop=False)
                        if d % RB == 0:
                            for m in range(2):
                                pe.wait_ge(s_qa[d // RB][m], (pp + 1) * (QUADS // 2) * 16)
                            pe.wait_ge(s_pa, (pp + 1) * QUADS)
                        for k in range(KT):
                            last = MM_(PS[:, 2 * (d % 2) + k, :], PA[:, k * P:(k + 1) * P], QA[:, t, bh * C:(bh + 1) * C],
                                       start=False, stop=True)
                        last.then_inc(s_fo, 1)

            pe.wait_ge(s_load, 16 * 8)
            pe.wait_ge(s_seta, 3)
            pe.wait_ge(s_one, 1)
            gavg(1)
            with pe.Fori(0, IMAGES) as img:
                for c in range(-1, NC + 4):
                    if 0 <= c - 5 < NC:
                        turn_q(img, c - 5)
                    d = c - 2
                    if 0 <= d < NC:
                        project0(img, d)
                    if c + 1 < NC:
                        total(img, c + 1, s_sqs, s_ss, s_ln)

                def turn_k(d):
                    pe.wait_ge(s_ke, img * EK + 1 + d // (NC // EK))
                    if d >= 2:
                        pe.wait_ge(s_ekt, img * NC + d - 1)
                    for j in range(4):
                        at = d * C + j * P
                        last = nc.tensor.transpose(PS[:, 2 + d % 2, j * P:(j + 1) * P], KBUF[:, at:at + P], ident)
                    last.then_inc(s_ket, 1)

                turn_k(0)
                turn_q(img, NC - 1)
                for d in range(NC):
                    if d + 1 < NC:
                        turn_k(d + 1)
                    pe.wait_ge(s_ekt, img * NC + d + 1)
                    for j in range(4):
                        at = d * C + j * P
                        last = MM_(PS[:, 7, 0:P], VT[:, at:at + P], EKT[:, d % 2, j, :], start=(d == 0 and j == 0),
                                   stop=(d == NC - 1 and j == 3))
                    last.then_inc(s_ctx, 1)
                pe.wait_ge(s_sm, img + 1)
                pe.wait_ge(s_qs, img * NC + NC)
                MM_(PS[:, 6, 0:CH], SM, WOUT[:, :], start=True, stop=True).then_inc(s_mp, 1)
                pe.wait_ge(s_mm, img + 1)
                for c in range(NC + 1):
                    if c < NC:
                        if c >= 2:
                            pe.wait_ge(s_ysq, img * 2 * NC + 2 * c - 2)
                        for k in range(KT):
                            last = MM_(PS[:, 2 + 2 * (c % 2) + k, :], MM[:, k * P:(k + 1) * P], QS[:, c * C:(c + 1) * C],
                                       start=True, stop=True)
                        last.then_inc(s_y, 1)
                    if c >= 1:
                        total(img, c - 1, s_ysqs, s_yss, s_yln)
                gavg(img * 2 + 2)
                with pe.Fori(0, PAIRS - 1) as pair:
                    attend1(img, pair)
                    finish(img, img * PAIRS + pair, False)
                attend1(img, PAIRS - 1)
                finish(img, img * PAIRS + PAIRS - 1, True)


def kernel(x, L0_conv_W_qkv, L0_conv_W_out, L0_conv_b_out, L0_conv_g_norm, L0_conv_g_out, L1_conv_w_qkv,
           L1_conv_w_dw, L1_conv_w_pw, L1_conv_w_proj, L1_conv_bn_gamma, L1_conv_bn_beta, L1_conv_bn_mean,
           L1_conv_bn_var):
    import concourse.bacc as bacc
    from concourse.bass_utils import run_bass_kernel_spmd

    kind = [1, 2, 0]
    heads = 4 * QUADS
    by_tile = np.array([[[3 * (p * heads + h) + kind[ty] for h in range(heads)] for ty in range(TY)]
                        for p in range(PAIRS)])
    by_conv = by_tile.reshape(PAIRS, TY, QUADS, 4).transpose(0, 2, 1, 3).reshape(-1)
    w1 = np.asarray(L1_conv_w_qkv).reshape(96, 8, CH)[by_tile.reshape(-1)].reshape(768, CH)
    pw = np.asarray(L1_conv_w_pw)[by_conv]
    pwp = np.broadcast_to(pw.transpose(2, 0, 1)[None, :, None, None], (2, 8, 2, 4, 96, 8)).reshape(P, -1)
    dw = np.asarray(L1_conv_w_dw).reshape(96, 8, TAPS, TAPS)[by_conv]
    dwp = np.zeros((2, 8, 2, 4, 96, TAPS, RB), np.float32)
    for half in range(2):
        for t in range(4):
            for row in range(RB):
                dy = 4 * half + t - row
                if 0 <= dy < TAPS:
                    dwp[half, :, :, t, :, :, row] = dw[:, :, dy, :].transpose(1, 0, 2)[:, None]
    wp = np.asarray(L1_conv_w_proj).T.reshape(2, PAIRS, P, CH)
    wpa = np.repeat(wp[1].reshape(PAIRS * QUADS, 32, 1, CH), RB, axis=2).reshape(PAIRS * QUADS, P, CH)
    vecs = np.stack([np.asarray(v).reshape(KT, P).T for v in (
        L0_conv_g_norm, L0_conv_b_out, L0_conv_g_out, L1_conv_bn_gamma, L1_conv_bn_beta, L1_conv_bn_mean,
        L1_conv_bn_var)], axis=1)
    arrays = {
        "x": np.asarray(x).reshape(IMAGES, CH, N), "cst": constants(),
        "w0t": np.asarray(L0_conv_W_qkv).T, "vecs": vecs,
        "woutt": np.asarray(L0_conv_W_out).T, "w1t": w1.T, "pwp": pwp, "dwp": dwp.reshape(P, -1), "wpd": wp[0],
        "wpa": wpa,
    }
    nc = bacc.Bacc("TRN2", target_bir_lowering=False, num_devices=1)
    args, given = [], {}
    for name, a in arrays.items():
        a = np.ascontiguousarray(a)
        given["in_" + name] = a
        args.append(nc.dram_tensor("in_" + name, a.shape, mybir.dt.from_np(a.dtype), kind="ExternalInput").ap())
    args.append(nc.dram_tensor("out_y", (IMAGES, CH, N), F32, kind="ExternalOutput").ap())
    two_layers(nc, *args)
    r = run_bass_kernel_spmd(nc, [given], core_ids=[0])
    return r.results[0]["out_y"].reshape(IMAGES, CH, H, W)
```
